# Optimizing a Trainium2 kernel written in Bass

```python
import numpy as np
import jax
import jax.numpy as jnp

def _softmax(x, axis=-1):
    return jax.nn.softmax(x, axis=axis)

def _gelu(x):
    return jax.nn.gelu(x, approximate=True)

def _silu(x):
    return jax.nn.silu(x)

def _sigmoid(x):
    return jax.nn.sigmoid(x)

def _layernorm(x, axis=-1, eps=1e-05):
    m = jnp.mean(x, axis=axis, keepdims=True)
    v = jnp.var(x, axis=axis, keepdims=True)
    return (x - m) / jnp.sqrt(v + eps)

def _scatter_add(tgt, idx, src, axis=0):
    return tgt.at[idx].add(src)

def _segment_sum(src, seg, n):
    return jax.ops.segment_sum(src, seg, n)
kernel_name = 'mk_adj_ffn_d1_adj_r2_6966b3'

def setup_inputs(seed: int=0):
    np.random.seed(seed)
    _w = jnp.asarray

    def _rec_inputs():
        import jax
        import jax.numpy as jnp
        _gk = jax.random.key(seed)
        x = -0.0003929 + 0.9999 * jax.random.normal(jax.random.fold_in(_gk, 1), (32, 256, 256), jnp.float32)
        _a = jax.random.bernoulli(jax.random.fold_in(_gk, 2), 0.0078125, (32, 256, 256))
        _a = jnp.logical_or(_a, jnp.swapaxes(_a, -1, -2))
        _a = jnp.logical_or(_a, jnp.eye(256, dtype=bool))
        _af = _a.astype(jnp.float32)
        _af = _af * jax.random.uniform(jax.random.fold_in(_gk, 3), (32, 256, 256), jnp.float32, 0.05, 1)
        adj = _af
        return (x, adj)
    x, adj = _rec_inputs()

    def _L0_gnn_setup():
        import jax, jax.numpy as jnp
        import numpy as np
        B, N, F_IN, F_HID, F_OUT = (32, 512, 256, 256, 256)

        def _gcn_layer(x, adj, W, b):
            support = jnp.einsum('bnf,fh->bnh', x, W)
            return jnp.einsum('bnm,bmh->bnh', adj, support) + b
        key = jax.random.key(seed)
        ks = jax.random.split(key, 8)

        def xavier(k, fan_in, fan_out):
            bound = float(np.sqrt(6.0 / (fan_in + fan_out)))
            return jax.random.uniform(k, (fan_in, fan_out), jnp.float32, -bound, bound)
        return {'batch_graph': jax.random.normal(ks[0], (B, N, F_IN), jnp.float32), 'adj': jax.random.uniform(ks[1], (B, N, N), jnp.float32), 'W1': xavier(ks[2], F_IN, F_HID), 'b1': jnp.zeros((F_HID,), jnp.float32), 'W2': xavier(ks[3], F_HID, F_HID), 'b2': jnp.zeros((F_HID,), jnp.float32), 'W3': xavier(ks[4], F_HID, F_OUT), 'b3': jnp.zeros((F_OUT,), jnp.float32)}
    _L0_gnn_all = _L0_gnn_setup()
    _L0_gnn_in = {k: v for k, v in _L0_gnn_all.items() if k in ('W1', 'b1', 'W2', 'b2', 'W3', 'b3')}
    del _L0_gnn_all

    def _L0_ffn_setup():
        import jax, jax.numpy as jnp
        import numpy as np
        D_MODEL = 256
        D_FF = 1024
        N_EXPERTS = 64
        K_ACTIVE = 2
        N_HASHES = 4
        LAYER_ID = 0
        SALT = 0.0
        BUCKET_SCALE = 8.0
        CAPACITY_FACTOR = 1.25
        key = jax.random.key(seed)
        k0, k1, k2, k3 = jax.random.split(key, 4)
        B, S = (4, 1024)
        hidden_states = jax.random.normal(k0, (B, S, D_MODEL), dtype=jnp.float32)
        W_hash = jax.random.normal(k1, (N_HASHES, D_MODEL), dtype=jnp.float32) / np.float32(np.sqrt(D_MODEL))
        W1 = jax.random.normal(k2, (N_EXPERTS, D_MODEL, D_FF), dtype=jnp.float32) * np.float32(1.0 / np.sqrt(D_MODEL))
        b1 = jnp.zeros((N_EXPERTS, D_FF), dtype=jnp.float32)
        W2 = jax.random.normal(k3, (N_EXPERTS, D_FF, D_MODEL), dtype=jnp.float32) * np.float32(1.0 / np.sqrt(D_FF))
        b2 = jnp.zeros((N_EXPERTS, D_MODEL), dtype=jnp.float32)
        return {'hidden_states': hidden_states, 'W_hash': W_hash, 'W1': W1, 'b1': b1, 'W2': W2, 'b2': b2}
    _L0_ffn_all = _L0_ffn_setup()
    _L0_ffn_in = {k: v for k, v in _L0_ffn_all.items() if k in ('W_hash', 'W1', 'b1', 'W2', 'b2')}
    del _L0_ffn_all
    return {'x': x, 'adj': adj, 'L0_gnn_W1': _L0_gnn_in['W1'], 'L0_gnn_b1': _L0_gnn_in['b1'], 'L0_gnn_W2': _L0_gnn_in['W2'], 'L0_gnn_b2': _L0_gnn_in['b2'], 'L0_gnn_W3': _L0_gnn_in['W3'], 'L0_gnn_b3': _L0_gnn_in['b3'], 'L0_ffn_W_hash': _L0_ffn_in['W_hash'], 'L0_ffn_W1': _L0_ffn_in['W1'], 'L0_ffn_b1': _L0_ffn_in['b1'], 'L0_ffn_W2': _L0_ffn_in['W2'], 'L0_ffn_b2': _L0_ffn_in['b2']}

def reference(x, adj, L0_gnn_W1, L0_gnn_b1, L0_gnn_W2, L0_gnn_b2, L0_gnn_W3, L0_gnn_b3, L0_ffn_W_hash, L0_ffn_W1, L0_ffn_b1, L0_ffn_W2, L0_ffn_b2):
    import jax
    import jax.numpy as jnp

    def _L0_gnn_ref(batch_graph, adj, W1, b1, W2, b2, W3, b3):
        import jax, jax.numpy as jnp
        import numpy as np
        B, N, F_IN, F_HID, F_OUT = (32, 512, 256, 256, 256)

        def _gcn_layer(x, adj, W, b):
            support = jnp.einsum('bnf,fh->bnh', x, W)
            return jnp.einsum('bnm,bmh->bnh', adj, support) + b
        x = jax.nn.relu(_gcn_layer(batch_graph, adj, W1, b1))
        x = jax.nn.relu(_gcn_layer(x, adj, W2, b2))
        out = _gcn_layer(x, adj, W3, b3)
        return out

    def _L0_ffn_ref(hidden_states, W_hash, W1, b1, W2, b2):
        import jax, jax.numpy as jnp
        import numpy as np
        D_MODEL = 256
        D_FF = 1024
        N_EXPERTS = 64
        K_ACTIVE = 2
        N_HASHES = 4
        LAYER_ID = 0
        SALT = 0.0
        BUCKET_SCALE = 8.0
        CAPACITY_FACTOR = 1.25
        B, S, D = hidden_states.shape
        T = B * S
        x = hidden_states.reshape(T, D)
        scores = x @ W_hash.T
        buckets = jnp.mod(jnp.floor(scores * BUCKET_SCALE + SALT).astype(jnp.int32) + LAYER_ID, N_EXPERTS)
        selected = buckets[:, :K_ACTIVE]
        flat_e = selected.reshape(-1)
        C = int(np.ceil(T * K_ACTIVE / N_EXPERTS * CAPACITY_FACTOR))
        oh = jax.nn.one_hot(flat_e, N_EXPERTS, dtype=jnp.int32)
        pos = jnp.sum((jnp.cumsum(oh, axis=0) - 1) * oh, axis=1)
        valid = pos < C
        pos_c = jnp.clip(pos, 0, C - 1)
        x_rep = jnp.repeat(x, K_ACTIVE, axis=0)
        buf = jnp.zeros((N_EXPERTS, C, D), dtype=x.dtype).at[flat_e, pos_c].add(jnp.where(valid[:, None], x_rep, 0.0))
        h = jax.nn.gelu(jnp.einsum('ecd,edf->ecf', buf, W1) + b1[:, None, :], approximate=False)
        y = jnp.einsum('ecf,efd->ecd', h, W2) + b2[:, None, :]
        out_pairs = jnp.where(valid[:, None], y[flat_e, pos_c], 0.0)
        out = out_pairs.reshape(T, K_ACTIVE, D).mean(axis=1)
        return out.reshape(B, S, D)
    x = x + _L0_gnn_ref(_layernorm(x, axis=-1), adj, L0_gnn_W1, L0_gnn_b1, L0_gnn_W2, L0_gnn_b2, L0_gnn_W3, L0_gnn_b3)
    x = x + _L0_ffn_ref(_layernorm(x, axis=-1), L0_ffn_W_hash, L0_ffn_W1, L0_ffn_b1, L0_ffn_W2, L0_ffn_b2)
    return x

_drawn_inputs = setup_inputs


def setup_inputs(seed=0):
    import zlib

    import numpy as np

    out = dict(_drawn_inputs(seed))
    spreads = {'L0_gnn_b1': (0.0, 0.1),
     'L0_gnn_b2': (0.0, 0.1),
     'L0_gnn_b3': (0.0, 0.1),
     'L0_ffn_b1': (0.0, 0.8),
     'L0_ffn_b2': (0.0, 0.761)}
    factors = {}
    for name, (base, spread) in spreads.items():
        noise = np.random.default_rng([zlib.crc32(name.encode()), seed]).standard_normal(out[name].shape)
        drawn = base * np.exp(spread * noise) if base else spread * noise
        out[name] = jnp.asarray(drawn.astype(out[name].dtype))
    for name, factor in factors.items():
        out[name] = (out[name] * factor).astype(out[name].dtype)
    return out
```

```python
import concourse.bass as bass
from concourse import mybir
from contextlib import ExitStack


def gnn_then_hash_routed_experts(
    nc: bass.Bass,
    x: bass.AP,
    adj: bass.AP,
    gw1: bass.AP,
    gb1: bass.AP,
    gw2: bass.AP,
    gb2: bass.AP,
    gw3: bass.AP,
    gb3: bass.AP,
    w_hash: bass.AP,
    ew1: bass.AP,
    eb1: bass.AP,
    ew2: bass.AP,
    eb2: bass.AP,
    out: bass.AP,
):
    fp32 = mybir.dt.float32
    bf16 = mybir.dt.bfloat16
    i32 = mybir.dt.int32
    ALU = mybir.AluOpType
    ACT = mybir.ActivationFunctionType
    AX = mybir.AxisListType

    P = 128
    B, N, D = x.shape
    E, _, F = ew1.shape
    K = 2
    T = B * N
    CAP = -(-(T * K * 5) // (E * 4))
    EPS = 1e-5
    BUCKET_SCALE = 8.0

    PAIRS = B // 2
    TPP = 2 * N // P
    KD = D // P
    NT = T // P
    JF = F // P
    WIDTHS = [128, 192, 256, CAP]
    FILL = P
    STRIDE = CAP + FILL
    CB = -(-CAP // P)
    ROW = D + 4
    NONE = float(1 << 20)
    U = 4
    HALF = E // 2
    LOADED = 16
    SENT = 48
    G = 4
    LAST = NT // G
    ZROWS = 8

    def blocks(w):
        return [(c, min(P, w - c * P)) for c in range(-(-w // P))]

    rows_hbm = nc.dram_tensor("expert_rows", (E * STRIDE, ROW), fp32, kind="Internal").ap()
    pairs_hbm = nc.dram_tensor("pair_results", (T * K, D), fp32, kind="Internal").ap()
    x_tok = x.rearrange("b n d -> (b n) d")
    adj_tok = adj.rearrange("b n m -> (b n) m")
    out_tok = out.rearrange("b n d -> (b n) d")

    ctx = ExitStack()
    with ctx:
        def sb(name, shape, dt=fp32):
            return ctx.enter_context(nc.sbuf_tensor(name, shape, dt))

        def sem(name):
            return ctx.enter_context(nc.semaphore(name))

        ident = sb("ident", [P, P])
        ones_f = sb("ones_f", [P, P])
        ones_b = sb("ones_b", [P, P], bf16)
        before = sb("before", [P, P], bf16)
        expert_no = sb("expert_no", [P, E])
        pair_id = sb("pair_id", [P, PAIRS, K, TPP], i32)
        gw1_sb = sb("gw1_sb", [P, KD, D])
        gw2_sb = sb("gw2_sb", [P, KD, D])
        gw3_sb = sb("gw3_sb", [P, KD, D])
        gb1_sb = sb("gb1_sb", [P, KD])
        gb2_sb = sb("gb2_sb", [P, KD])
        gb3_bc = sb("gb3_bc", [P, D])
        hash_bc = sb("hash_bc", [P, K, D])
        eb1_t = sb("eb1_t", [P, JF, E])
        empty_row = sb("empty_row", [FILL, ROW])
        x1 = sb("x1", [P, NT, D])
        x_in = sb("x_in", [P, TPP, D])
        adj_in = sb("adj_in", [P, TPP, N])
        xn = sb("xn", [P, TPP, D])
        adj_t = sb("adj_t", [P, 2, KD, N])
        y_t = sb("y_t", [P, 2, KD, N])
        h1_t = sb("h1_t", [P, 2, KD, N])
        s2 = sb("s2", [P, 2, KD, D])
        h2_t = sb("h2_t", [P, 2, KD, N])
        s3 = sb("s3", [P, 2, KD, D])
        stats = sb("stats", [P, TPP, 6])
        mv = sb("mv", [P, TPP, 2])
        var_e = sb("var_e", [P, TPP])
        minus_half = sb("minus_half", [P, TPP])
        rstd = sb("rstd", [P, 4, TPP])
        payload = sb("payload", [P, K, TPP, ROW])
        score = sb("score", [P, K * TPP])
        floor_i = sb("floor_i", [P, 3, K * TPP], i32)
        floor_f = sb("floor_f", [P, 3, K * TPP])
        bucket = sb("bucket", [P, K * TPP])
        same = sb("same", [P, TPP])
        onehot = sb("onehot", [P, K, TPP, E], bf16)
        tile_cnt = sb("tile_cnt", [P, TPP, E], bf16)
        two_cnt = sb("two_cnt", [P, 2, E], bf16)
        run_cnt = sb("run_cnt", [P, E], bf16)
        pos = sb("pos", [P, 3, K * TPP])
        slot = sb("slot", [P, K * TPP], i32)
        count = sb("count", [P, E], i32)
        w1_sb = sb("w1_sb", [P, 2, KD, F])
        w2_sb = sb("w2_sb", [P, 2, JF, D])
        eb2_bc = sb("eb2_bc", [P, 2, D])
        xr = sb("xr", [P, U, CB, ROW])
        xt_words = sb("xt_words", [P, 2 * KD * CAP])
        h_words = sb("h_words", [P, 2 * JF * CAP])
        y_words = sb("y_words", [P, 2 * CB * D])
        xt = xt_words[:, :].rearrange("p (s k c) -> p s k c", s=2, k=KD)
        h_t = h_words[:, :].rearrange("p (s j c) -> p s j c", s=2, j=JF)
        y_out = y_words[:, :].rearrange("p (s c d) -> p s c d", s=2, c=CB)
        xb3 = xt_words[:, 0:TPP * D].rearrange("p (t d) -> p t d", t=TPP)
        eb1_in = y_words[0:E, 0:F]
        zeros = h_words[:, 0:ZROWS * D]
        prod = h_words[:, ZROWS * D:ZROWS * D + K * TPP * D].rearrange("p (c d) -> p c d", d=D)
        picked = h_words[:, ZROWS * D + K * TPP * D:ZROWS * D + K * TPP * (D + E)]
        pr_in = h_words[:, 0:2 * G * K * D].rearrange("p (s t k d) -> p s t k d", s=2, t=G, k=K)

        ps = ctx.enter_context(nc.psum_tensor("ps", [P, 8, 512], fp32))
        T_BANK, Y_BANK, H1_BANK, S2_BANK, H2_BANK, S3_BANK, O3_BANK = 0, 1, 2, 3, 0, 1, 2
        PREFIX = ps[:, 3, 0:TPP * E]
        COUNTS = ps[:, 7, 0:E]
        XT_BANKS, H_BANK, H_BANKS, Y_BANK2 = ps[:, 0:2, :], 2, 4, 6

        def bank(b, g):
            return ps[:, 4 * g + b, :].rearrange("p (k n) -> p k n", k=2)

        def y_bank(c, m):
            return ps[0:m, Y_BANK2 + c // 2, (c % 2) * D:(c % 2) * D + D]

        S = {n: sem(n) for n in """
            adj_loaded x_loaded consts_in eb1_loaded consts_made
            adj_t_ps y_ps h1_ps s2_ps h2_ps s3_ps o3_ps
            adj_t_sb y_sb h1_sb s2_sb h2_sb s3_sb x1_made
            xn_made xb3_made x_free var_made rough_made cnt_made prefix_ps prefix_read run_made
            slots_made rows_sent pairs_zeroed total_ps count_made b1_ps b1_sb dve_step pool_step
            xt_ps xt_sb hid_ps hid_sb down_done y_made summed stored passed""".split()}
        y_sent = [sem(f"y_sent{u}") for u in range(U)]
        filled = [sem(f"filled{u}") for u in range(U)]
        xr_loaded = [sem(f"xr_loaded{u}") for u in range(U)]
        w1_loaded = [sem(f"w1_loaded{s}") for s in range(2)]
        w2_loaded = [sem(f"w2_loaded{s}") for s in range(2)]
        b2_loaded = [sem(f"b2_loaded{s}") for s in range(2)]
        pr_loaded = [sem(f"pr_loaded{s}") for s in range(2)]
        N_CONSTS = 8

        block = ctx.enter_context(nc.Block())

        def expert(j, u):
            return 2 * j + u // 2 + HALF * (u % 2)

        def later(j, u, d):
            return j + (u + d) // U, (u + d) % U

        def uses(j, u):
            return 2 * j + u // 2 + 1

        def rounds_sent(eng, j, u, d):
            at, place = later(j, u, d)
            eng.wait_ge(y_sent[place], SENT * (at + 1))

        def rows_of(eng, j, u):
            return eng.value_load(count[0:1, bass.ds(expert(j, u), 1)], min_val=0, max_val=CAP)

        def by_width(eng, n, body):
            with eng.If(n < WIDTHS[0] + 1):
                body(WIDTHS[0])
            with eng.Else():
                with eng.If(n < WIDTHS[2] + 1):
                    with eng.If(n < WIDTHS[1] + 1):
                        body(WIDTHS[1])
                    with eng.Else():
                        body(WIDTHS[2])
                with eng.Else():
                    body(WIDTHS[3])

        def rounds(eng, body):
            body(0)
            with eng.Fori(1, E // U - 1) as j:
                body(j)
            body(E // U - 1)

        def pairs(eng, body):
            body(0)
            with eng.Fori(1, PAIRS - 1) as i:
                body(i)
            body(PAIRS - 1)

        def passed(eng):
            eng.sem_inc(S["passed"], 1)

        def is_first(i):
            return isinstance(i, int) and i == 0

        def is_last(i, n):
            return isinstance(i, int) and i == n - 1

        @block.sync
        def _(sp):
            def load_x(i):
                sp.dma_start(x_in[:, :, :], x_tok[bass.ds(i * 2 * N, 2 * N), :].rearrange(
                    "(t p) d -> p t d", p=P)).then_inc(S["x_loaded"], 16)

            def load_adj(i):
                sp.dma_start(adj_in[:, :, :], adj_tok[bass.ds(i * 2 * N, 2 * N), :].rearrange(
                    "(t p) d -> p t d", p=P)).then_inc(S["adj_loaded"], 16)

            def zero_pairs(i):
                sp.dma_start(pairs_hbm[bass.ds(i * P * ZROWS, P * ZROWS), :].rearrange(
                    "(p r) d -> p (r d)", p=P), zeros).then_inc(S["pairs_zeroed"], 16)

            def load_w1(j, u):
                sp.dma_start(w1_sb[:, u % 2, :, :], ew1[expert(j, u)].rearrange(
                    "(k p) f -> p k f", p=P)).then_inc(w1_loaded[u % 2], 16)

            def load_w2(j, u):
                sp.dma_start(w2_sb[:, u % 2, :, :], ew2[expert(j, u)].rearrange(
                    "(f p) d -> p f d", p=P)).then_inc(w2_loaded[u % 2], 16)

            def load_b2(j, u):
                sp.dma_start(eb2_bc[:, u % 2, :], eb2[expert(j, u), :].partition_broadcast(
                    P)).then_inc(b2_loaded[u % 2], 16)

            load_adj(0)
            load_x(0)
            sp.dma_start(gw1_sb[:, :, :], gw1.rearrange("(k p) d -> p k d", p=P)).then_inc(S["consts_in"], 16)
            with nc.allow_non_contiguous_dma(reason="256 bias values, once"):
                sp.dma_start(gb1_sb[:, :], gb1.rearrange("(k p) -> p k", p=P)).then_inc(S["consts_in"], 16)
                sp.dma_start(gb2_sb[:, :], gb2.rearrange("(k p) -> p k", p=P)).then_inc(S["consts_in"], 16)
            sp.dma_start(gw2_sb[:, :, :], gw2.rearrange("(k p) d -> p k d", p=P)).then_inc(S["consts_in"], 16)
            sp.dma_start(gw3_sb[:, :, :], gw3.rearrange("(k p) d -> p k d", p=P)).then_inc(S["consts_in"], 16)
            sp.dma_start(gb3_bc[:, :], gb3.partition_broadcast(P)).then_inc(S["consts_in"], 16)
            for k in range(K):
                sp.dma_start(hash_bc[:, k, :], w_hash[k, :].partition_broadcast(P)).then_inc(S["consts_in"], 16)
            sp.dma_start(eb1_in, eb1).then_inc(S["eb1_loaded"], 16)
            sp.wait_ge(S["consts_made"], 1)
            with sp.Fori(1, PAIRS) as i:
                sp.wait_ge(S["adj_t_ps"], 2 * i)
                load_adj(i)
                sp.wait_ge(S["x_free"], 2 * i)
                load_x(i)
                zero_pairs(i - 1)
            zero_pairs(PAIRS - 1)
            for u in range(2):
                load_w1(0, u)
                load_w2(0, u)
                load_b2(0, u)

            def fill(j, u):
                n = rows_of(sp, j, u)
                sp.dma_start(rows_hbm[bass.ds(expert(j, u) * STRIDE + n, FILL), :],
                             empty_row[:, :]).then_inc(filled[u], 16)

            def load_rows(j, u):
                n = rows_of(sp, j, u)
                row = expert(j, u) * STRIDE
                sp.wait_ge(filled[u], 16 * (j + 1))
                passed(sp)

                def body(w):
                    full, rest = w // P, w % P
                    if full:
                        sp.dma_start(xr[:, u, 0:full, :], rows_hbm[bass.ds(row, full * P), :].rearrange(
                            "(c p) d -> p c d", p=P)).then_inc(xr_loaded[u], 16 if rest else 32)
                    if rest:
                        sp.dma_start(xr[0:rest, u, full, :], rows_hbm[bass.ds(
                            row + full * P, rest), :]).then_inc(xr_loaded[u], 16 if full else 32)
                by_width(sp, n, body)

            sp.wait_ge(S["count_made"], 1)
            fill(0, 0)
            fill(0, 1)
            sp.wait_ge(S["rows_sent"], 16 * K * NT)
            load_rows(0, 0)

            def round_of_loads(j):
                for u in range(U):
                    i = U * j + u
                    if not (is_last(j, E // U) and u >= 2):
                        fill(*later(j, u, 2))
                    if not (is_first(j) and u < 2):
                        sp.wait_ge(S["hid_ps"], JF * (i - 1))
                        load_w1(j, u)
                    if not (is_last(j, E // U) and u == 3):
                        if not (is_first(j) and u < 3):
                            rounds_sent(sp, j, u, -3)
                            passed(sp)
                        load_rows(*later(j, u, 1))
                    if not (is_first(j) and u < 2):
                        sp.wait_ge(S["down_done"], i - 1)
                        load_w2(j, u)
                        sp.wait_ge(S["y_made"], i - 1)
                        load_b2(j, u)
            rounds(sp, round_of_loads)

            for u in range(U):
                sp.wait_ge(y_sent[u], SENT * (E // U))
            pair_rows = pairs_hbm.rearrange("(t k) d -> t (k d)", k=K)
            with sp.Fori(0, LAST // 2) as q:
                for s in range(2):
                    sp.wait_ge(S["summed"], 2 * q + s + 1)
                    sp.dma_start(pr_in[:, s, :, :, :].rearrange("p t k d -> p t (k d)"),
                                 pair_rows[bass.ds((2 * q + s) * G * P, G * P), :].rearrange(
                                     "(t p) d -> p t d", p=P)).then_inc(pr_loaded[s], 16)

        @block.gpsimd
        def _(pool):
            nc.gpsimd.memset(ones_f[:, :], 1.0)
            nc.gpsimd.memset(ones_b[:, :], 1.0)
            nc.gpsimd.memset(run_cnt[:, :], 0.0)
            nc.gpsimd.memset(minus_half[:, :], -0.5)
            nc.gpsimd.memset(zeros, 0.0)
            nc.gpsimd.memset(payload[:, :, :, :], 0.0)
            nc.gpsimd.memset(empty_row[:, :], 0.0).then_inc(S["pool_step"], 1)
            pool.wait_ge(S["pool_step"], 1)
            nc.gpsimd.memset(empty_row[:, D:D + 1].bitcast(i32), T * K)
            nc.gpsimd.affine_select(out=ident[:, :], in_=ones_f[:, :], compare_op=ALU.is_equal, fill=0.0, base=0,
                                    pattern=[[-1, P]], channel_multiplier=1)
            nc.gpsimd.affine_select(out=before[:, :], in_=ones_b[:, :], compare_op=ALU.is_gt, fill=0.0, base=0,
                                    pattern=[[1, P]], channel_multiplier=-1)
            nc.gpsimd.iota(expert_no[:, :], pattern=[[1, E]], base=0, channel_multiplier=0,
                           allow_small_or_imprecise_dtypes=True)
            nc.gpsimd.iota(pair_id[:, :, :, :], pattern=[[TPP * P * K, PAIRS], [1, K], [P * K, TPP]], base=0,
                           channel_multiplier=K).then_inc(S["consts_made"], 1)
            pool.wait_ge(S["consts_in"], 16 * N_CONSTS)

            def add_b3(i):
                pool.wait_ge(S["x_loaded"], 16 * (i + 1))
                if not is_first(i):
                    pool.wait_ge(S["x1_made"], 2 * i)
                nc.gpsimd.tensor_tensor(xb3, x_in[:, :, :], gb3_bc[:, :].unsqueeze(1).to_broadcast([P, TPP, D]),
                                        ALU.add).then_inc(S["xb3_made"], 1)
                pool.wait_ge(S["xb3_made"], i + 1)
                pool.sem_inc(S["x_free"], 1)

            def count_pair(i):
                pool.wait_ge(S["prefix_ps"], i + 1)
                nc.gpsimd.tensor_tensor(two_cnt[:, :, :], tile_cnt[:, 0:2, :], tile_cnt[:, 2:4, :],
                                        ALU.add).then_inc(S["pool_step"], 1)
                pool.wait_ge(S["pool_step"], 2 * i + 2)
                nc.gpsimd.tensor_tensor(run_cnt[:, :], run_cnt[:, :], two_cnt[:, 0, :], ALU.add).then_inc(S["pool_step"], 1)
                pool.wait_ge(S["pool_step"], 2 * i + 3)
                nc.gpsimd.tensor_tensor(run_cnt[:, :], run_cnt[:, :], two_cnt[:, 1, :], ALU.add).then_inc(S["run_made"], 1)
                pool.wait_ge(S["run_made"], i + 1)

            def send_rows(i):
                pool.wait_ge(S["slots_made"], i + 1)
                passed(pool)
                for k in range(K):
                    for t in range(TPP):
                        c = k * TPP + t
                        nc.gpsimd.indirect_dma_start(
                            out=rows_hbm, out_offset=bass.IndirectOffsetOnAxis(ap=slot[:, c:c + 1], axis=0),
                            in_=payload[:, k, t, :], in_offset=None, bounds_check=E * STRIDE - 1,
                            oob_is_err=False).then_inc(S["rows_sent"], 16)

            def rough_rstd(n):
                pool.wait_ge(S["var_made"], n)
                nc.gpsimd.tensor_tensor(rstd[:, 0, :], var_e[:, :], minus_half[:, :], ALU.pow).then_inc(
                    S["rough_made"], 1)

            rough_rstd(1)

            def pair_of_graphs(i):
                add_b3(i)
                if not is_first(i):
                    count_pair(i - 1)
                if not is_last(i, PAIRS):
                    rough_rstd(2 * i + 2)
                if not is_first(i):
                    send_rows(i - 1)
                rough_rstd(2 * i + 3 if not is_last(i, PAIRS) else 2 * PAIRS)
            pairs(pool, pair_of_graphs)
            count_pair(PAIRS - 1)
            send_rows(PAIRS - 1)

            pool.wait_ge(S["pairs_zeroed"], 16 * PAIRS)
            pool.wait_ge(S["count_made"], 1)

            def send_results(j, u):
                n = rows_of(pool, j, u)
                pool.wait_ge(S["y_made"], U * j + u + 1)
                passed(pool)

                def body(w):
                    cs = blocks(w)
                    for c, m in cs:
                        nc.gpsimd.indirect_dma_start(
                            out=pairs_hbm, out_offset=bass.IndirectOffsetOnAxis(
                                ap=xr[0:m, u, c, D:D + 1].bitcast(i32), axis=0),
                            in_=y_out[0:m, u % 2, c, :], in_offset=None, bounds_check=T * K - 1,
                            oob_is_err=False).then_inc(y_sent[u], SENT - 16 * (len(cs) - 1) if c == 0 else 16)
                by_width(pool, n, body)

            with pool.Fori(0, E // U) as j:
                for u in range(U):
                    send_results(j, u)

        @block.scalar
        def _(act):
            act.wait_ge(S["consts_in"], 16 * N_CONSTS)

            def out_of_psum(to, frm, ready, done, g_no):
                act.wait_ge(ready, g_no + 1)
                nc.scalar.copy(to, frm).then_inc(done, 1)

            def relu_out(to, g, b, bias, ready, done, g_no):
                act.wait_ge(ready, g_no + 1)
                for hb in range(KD):
                    last = nc.scalar.activation(to[:, g, hb, :], bank(b, g)[:, hb, :], ACT.Relu,
                                                bias=bias[:, hb:hb + 1])
                last.then_inc(done, 1)

            act.wait_ge(S["b1_ps"], 1)
            nc.scalar.copy(eb1_t[:, :, :].rearrange("p f e -> p (f e)"), ps[:, 3, :]).then_inc(S["b1_sb"], 1)

            def pair_of_graphs(i):
                for g in range(2):
                    if not is_first(i):
                        act.wait_ge(S["o3_ps"], 2 * (i - 1) + g + 1)
                    out_of_psum(adj_t[:, g, :, :], bank(T_BANK, g), S["adj_t_ps"], S["adj_t_sb"], 2 * i + g)
                for g in range(2):
                    out_of_psum(y_t[:, g, :, :], bank(Y_BANK, g), S["y_ps"], S["y_sb"], 2 * i + g)
                for g in range(2):
                    relu_out(h1_t, g, H1_BANK, gb1_sb, S["h1_ps"], S["h1_sb"], 2 * i + g)
                for g in range(2):
                    out_of_psum(s2[:, g, :, :], bank(S2_BANK, g), S["s2_ps"], S["s2_sb"], 2 * i + g)
                for g in range(2):
                    relu_out(h2_t, g, H2_BANK, gb2_sb, S["h2_ps"], S["h2_sb"], 2 * i + g)
                for g in range(2):
                    out_of_psum(s3[:, g, :, :], bank(S3_BANK, g), S["s3_ps"], S["s3_sb"], 2 * i + g)
            pairs(act, pair_of_graphs)

            act.wait_ge(S["count_made"], 1)
            act.wait_ge(S["b1_sb"], 1)

            def round_of_gelus(j):
                for u in range(U):
                    i = U * j + u
                    n = rows_of(act, j, u)
                    if not (is_first(j) and u < 2):
                        act.wait_ge(S["down_done"], i - 1)
                        passed(act)
                    bias = bass.ds(expert(j, u), 1)

                    def body(w):
                        for f in range(JF):
                            act.wait_ge(S["hid_ps"], JF * i + f + 1)
                            nc.scalar.activation(h_t[:, u % 2, f, 0:w], ps[:, H_BANK + f % H_BANKS, 0:w], ACT.Gelu,
                                                 bias=eb1_t[:, f, bias]).then_inc(S["hid_sb"], 1)
                    by_width(act, n, body)
            rounds(act, round_of_gelus)

            with act.Fori(0, LAST) as q:
                act.wait_ge(S["summed"], q + 3)
                act.dma_start(out_tok[bass.ds(q * G * P, G * P), :].rearrange("(t p) d -> p t d", p=P),
                              x1[:, bass.ds(q * G, G), :]).then_inc(S["stored"], 16)
            act.wait_ge(S["stored"], 16 * LAST)

        @block.vector
        def _(dve):
            PER_PAIR = 6 + 17 + 3
            made = {"base": 0, "n": 0}

            def step(ins):
                made["n"] += 1
                ins.then_inc(S["dve_step"], 1)
                dve.wait_ge(S["dve_step"], made["base"] + made["n"])

            def norm_scale(src, n_norm):
                for t in range(TPP):
                    last = nc.vector.bn_stats(stats[:, t, :], src(t))
                step(last)
                passed(dve)
                for t in range(TPP):
                    last = nc.vector.bn_aggr(mv[:, t, :], stats[:, t, :])
                step(last)
                nc.vector.tensor_scalar(var_e[:, :], mv[:, :, 1], EPS, None, ALU.add).then_inc(S["var_made"], 1)
                dve.wait_ge(S["rough_made"], n_norm)
                step(nc.vector.tensor_tensor(rstd[:, 1, :], rstd[:, 0, :], rstd[:, 0, :], ALU.mult))
                step(nc.vector.tensor_tensor(rstd[:, 2, :], rstd[:, 1, :], var_e[:, :], ALU.mult))
                step(nc.vector.tensor_scalar(rstd[:, 1, :], rstd[:, 2, :], -0.5, 1.5, ALU.mult, ALU.add))
                step(nc.vector.tensor_tensor(rstd[:, 3, :], rstd[:, 0, :], rstd[:, 1, :], ALU.mult))

            def first_norm(i, n_norm):
                dve.wait_ge(S["x_loaded"], 16 * (i + 1))
                norm_scale(lambda t: x_in[:, t, :], n_norm)
                if not is_first(i):
                    dve.wait_ge(S["y_ps"], 2 * i)
                for t in range(TPP):
                    last = nc.vector.tensor_scalar(xn[:, t, :], x_in[:, t, :], mv[:, t, 0:1], rstd[:, 3, t:t + 1],
                                                   ALU.subtract, ALU.mult)
                last.then_inc(S["xn_made"], 1)
                dve.wait_ge(S["xn_made"], i + 1)
                dve.sem_inc(S["x_free"], 1)

            def residual(i):
                dve.wait_ge(S["xb3_made"], i + 1)
                for g in range(2):
                    dve.wait_ge(S["o3_ps"], 2 * i + g + 1)
                    nc.vector.tensor_tensor(x1[:, bass.ds(TPP * i + 2 * g, 2), :], bank(O3_BANK, g),
                                            xb3[:, 2 * g:2 * g + 2, :], ALU.add).then_inc(S["x1_made"], 1)
                dve.wait_ge(S["x1_made"], 2 * i + 2)
                passed(dve)

            def second_norm(i):
                norm_scale(lambda t: x1[:, bass.ds(TPP * i + t, 1), :], 2 * i + 3 if not is_last(i, PAIRS)
                           else 2 * PAIRS)
                if not is_first(i):
                    dve.wait_ge(S["rows_sent"], 16 * K * TPP * i)
                nc.vector.tensor_copy(payload[:, :, :, D:D + 1].rearrange("p k t o -> p k (t o)").bitcast(i32),
                                      pair_id[:, bass.ds(i, 1), :, :].rearrange("p o k t -> p (o k) t"))
                for t in range(TPP):
                    last = nc.vector.tensor_scalar(payload[:, 0, t, 0:D], x1[:, bass.ds(TPP * i + t, 1), :],
                                                   mv[:, t, 0:1], rstd[:, 3, t:t + 1], ALU.subtract, ALU.mult)
                step(last)
                nc.vector.tensor_copy(payload[:, 1, :, 0:D], payload[:, 0, :, 0:D])
                for k in range(K):
                    for t in range(TPP):
                        c = k * TPP + t
                        last = nc.vector.tensor_tensor_reduce(
                            out=prod[:, c, :], in0=payload[:, 0, t, 0:D], in1=hash_bc[:, k, :], scale=1.0,
                            scalar=0.0, op0=ALU.mult, op1=ALU.add, accum_out=score[:, c:c + 1])
                step(last)
                step(nc.vector.tensor_scalar(floor_i[:, 0, :], score[:, :], BUCKET_SCALE, None, ALU.mult))
                step(nc.vector.tensor_copy(floor_f[:, 0, :], floor_i[:, 0, :]))
                step(nc.vector.scalar_tensor_tensor(out=floor_f[:, 1, :], in0=score[:, :], scalar=BUCKET_SCALE,
                                                    in1=floor_f[:, 0, :], op0=ALU.mult, op1=ALU.is_lt))
                step(nc.vector.tensor_tensor(floor_f[:, 2, :], floor_f[:, 0, :], floor_f[:, 1, :], ALU.subtract))
                step(nc.vector.tensor_copy(floor_i[:, 1, :], floor_f[:, 2, :]))
                step(nc.vector.tensor_scalar(floor_i[:, 2, :], floor_i[:, 1, :], E - 1, None, ALU.bitwise_and))
                step(nc.vector.tensor_copy(bucket[:, :], floor_i[:, 2, :]))
                step(nc.vector.tensor_tensor(same[:, :], bucket[:, 0:TPP], bucket[:, TPP:2 * TPP], ALU.is_equal))
                step(nc.vector.tensor_tensor(
                    onehot[:, :, :, :].rearrange("p k t e -> p (k t) e"),
                    bucket[:, :].unsqueeze(2).to_broadcast([P, K * TPP, E]),
                    expert_no[:, :].unsqueeze(1).to_broadcast([P, K * TPP, E]), ALU.is_equal))
                if not is_first(i):
                    dve.wait_ge(S["run_made"], i)
                nc.vector.tensor_tensor(tile_cnt[:, :, :], onehot[:, 0, :, :], onehot[:, 1, :, :],
                                        ALU.add).then_inc(S["cnt_made"], 1)

            def slots(i):
                dve.wait_ge(S["prefix_ps"], i + 1)
                if not is_first(i):
                    dve.wait_ge(S["rows_sent"], 16 * K * TPP * i)
                nc.vector.tensor_tensor(
                    picked.rearrange("p (k c) -> p k c", k=K),
                    onehot[:, :, :, :].rearrange("p k t e -> p k (t e)"),
                    PREFIX.unsqueeze(1).to_broadcast([P, K, TPP * E]), ALU.mult).then_inc(S["prefix_read"], 1)
                dve.wait_ge(S["prefix_read"], i + 2)
                step(nc.vector.tensor_reduce(pos[:, 0, :], picked.rearrange("p (c e) -> p c e", e=E), AX.X, ALU.add))
                step(nc.vector.tensor_tensor(pos[:, 0, TPP:2 * TPP], pos[:, 0, TPP:2 * TPP], same[:, :], ALU.add))
                nc.vector.scalar_tensor_tensor(out=pos[:, 1, :], in0=bucket[:, :], scalar=float(STRIDE),
                                               in1=pos[:, 0, :], op0=ALU.mult, op1=ALU.add)
                step(nc.vector.tensor_scalar(pos[:, 2, :], pos[:, 0, :], float(CAP), NONE, ALU.is_ge, ALU.mult))
                nc.vector.tensor_tensor(slot[:, :], pos[:, 1, :], pos[:, 2, :], ALU.add).then_inc(S["slots_made"], 1)
                dve.wait_ge(S["slots_made"], i + 1)

            dve.sem_inc(S["prefix_read"], 1)
            first_norm(0, 1)

            def pair_of_graphs(i):
                at = made["n"]
                if not isinstance(i, int):
                    made["base"] = (i - 1) * PER_PAIR
                if not is_first(i):
                    slots(i - 1)
                if not is_last(i, PAIRS):
                    first_norm(i + 1, 2 * i + 2)
                residual(i)
                second_norm(i)
                if not isinstance(i, int):
                    assert made["n"] - at == PER_PAIR, (made["n"] - at, PER_PAIR)
                    made["base"], made["n"] = 0, made["n"] + (PAIRS - 3) * PER_PAIR
            pairs(dve, pair_of_graphs)
            slots(PAIRS - 1)

            dve.wait_ge(S["total_ps"], 1)
            nc.vector.tensor_scalar(count[:, :], COUNTS, float(CAP), None, ALU.min).then_inc(S["count_made"], 1)
            dve.wait_ge(S["count_made"], 1)

            def rows_out(j, u):
                i = U * j + u
                n = rows_of(dve, j, u)
                if not (is_first(j) and u < 2):
                    dve.wait_ge(S["hid_ps"], JF * (i - 1))
                    passed(dve)

                def body(w):
                    dve.wait_ge(S["xt_ps"], i + 1)
                    nc.vector.tensor_copy(xt[:, u % 2, :, 0:w], XT_BANKS[:, :, 0:w]).then_inc(S["xt_sb"], 1)
                by_width(dve, n, body)

            def results_out(j, u):
                i = U * j + u
                n = rows_of(dve, j, u)
                dve.wait_ge(b2_loaded[u % 2], 16 * uses(j, u))
                if not (is_first(j) and u < 2):
                    rounds_sent(dve, j, u, -2)
                passed(dve)

                def body(w):
                    dve.wait_ge(S["down_done"], i + 1)
                    for c, m in blocks(w):
                        last = nc.vector.tensor_tensor(y_out[0:m, u % 2, c, :], y_bank(c, m),
                                                       eb2_bc[0:m, u % 2, :], ALU.add)
                    last.then_inc(S["y_made"], 1)
                by_width(dve, n, body)

            rows_out(0, 0)
            rows_out(0, 1)

            def round_of_results(j):
                for u in range(U):
                    if not (is_last(j, E // U) and u >= 2):
                        rows_out(*later(j, u, 2))
                    results_out(j, u)
            rounds(dve, round_of_results)

            dve.sem_inc(S["summed"], 2)
            base = made["n"]
            with dve.Fori(0, LAST // 2) as q:
                for s in range(2):
                    dve.wait_ge(pr_loaded[s], 16 * (q + 1))
                    nc.vector.tensor_tensor(pr_in[:, s, :, 0, :], pr_in[:, s, :, 0, :], pr_in[:, s, :, 1, :],
                                            ALU.add).then_inc(S["dve_step"], 1)
                    dve.wait_ge(S["dve_step"], base + 2 * q + s + 1)
                    tiles = x1[:, bass.ds((2 * q + s) * G, G), :]
                    nc.vector.scalar_tensor_tensor(out=tiles, in0=pr_in[:, s, :, 0, :], scalar=1.0 / K, in1=tiles,
                                                   op0=ALU.mult, op1=ALU.add).then_inc(S["summed"], 1)

        @block.tensor
        def _(pe):
            pe.wait_ge(S["consts_made"], 1)
            pe.wait_ge(S["consts_in"], 16 * N_CONSTS)
            pe.wait_ge(S["eb1_loaded"], 16)

            def product(to, lhs, rhs, done):
                for b in range(KD):
                    for k in range(KD):
                        last = nc.tensor.matmul(to[:, b, :], lhs(k, b), rhs(k), start=(k == 0), stop=(k == KD - 1))
                last.then_inc(done, 1)

            def half(b):
                return slice(b * P, b * P + P)

            for f in range(JF):
                last = nc.tensor.transpose(ps[:, 3, f * E:f * E + E], eb1_in[:, f * P:f * P + P], ident[0:E, 0:E])
            last.then_inc(S["b1_ps"], 1)

            def prefix(i):
                pe.wait_ge(S["cnt_made"], i + 1)
                if not is_first(i):
                    pe.wait_ge(S["run_made"], i)
                nc.tensor.matmul(PREFIX, before[:, :], tile_cnt[:, :, :].rearrange("p t e -> p (t e)"),
                                 start=True, stop=False)
                for t in range(TPP - 1):
                    nc.tensor.matmul(PREFIX[:, (t + 1) * E:], ones_b[:, :],
                                     tile_cnt[:, t, :].unsqueeze(1).to_broadcast([P, TPP - 1 - t, E]),
                                     start=False, stop=False)
                nc.tensor.matmul(PREFIX, ones_b[:, :], run_cnt[:, :].unsqueeze(1).to_broadcast([P, TPP, E]),
                                 start=False, stop=True).then_inc(S["prefix_ps"], 1)

            def pair_of_graphs(i):
                for g in range(2):
                    if g == 0:
                        pe.wait_ge(S["adj_loaded"], 16 * (i + 1))
                    for mb in range(KD):
                        for nb in range(KD):
                            last = nc.tensor.transpose(bank(T_BANK, g)[:, mb, half(nb)],
                                                       adj_in[:, 2 * g + nb, half(mb)], ident[:, :])
                    last.then_inc(S["adj_t_ps"], 1)
                for g in range(2):
                    pe.wait_ge(S["xn_made"], i + 1)
                    pe.wait_ge(S["adj_t_sb"], 2 * i + g + 1)
                    product(bank(Y_BANK, g), lambda k, b: xn[:, 2 * g + k, half(b)],
                            lambda k: adj_t[:, g, k, :], S["y_ps"])
                for g in range(2):
                    pe.wait_ge(S["y_sb"], 2 * i + g + 1)
                    if not is_first(i):
                        pe.wait_ge(S["x1_made"], 2 * (i - 1) + g + 1)
                    product(bank(H1_BANK, g), lambda k, b: gw1_sb[:, k, half(b)],
                            lambda k: y_t[:, g, k, :], S["h1_ps"])
                for g in range(2):
                    pe.wait_ge(S["h1_sb"], 2 * i + g + 1)
                    if is_first(i):
                        pe.wait_ge(S["b1_sb"], 1)
                    elif g == 0:
                        pe.wait_ge(S["prefix_read"], i)
                    product(bank(S2_BANK, g), lambda k, b: h1_t[:, g, k, half(b)],
                            lambda k: gw2_sb[:, k, :], S["s2_ps"])
                for g in range(2):
                    pe.wait_ge(S["s2_sb"], 2 * i + g + 1)
                    product(bank(H2_BANK, g), lambda k, b: s2[:, g, k, half(b)],
                            lambda k: adj_t[:, g, k, :], S["h2_ps"])
                if not is_first(i):
                    prefix(i - 1)
                for g in range(2):
                    pe.wait_ge(S["h2_sb"], 2 * i + g + 1)
                    product(bank(S3_BANK, g), lambda k, b: h2_t[:, g, k, half(b)],
                            lambda k: gw3_sb[:, k, :], S["s3_ps"])
                for g in range(2):
                    pe.wait_ge(S["s3_sb"], 2 * i + g + 1)
                    product(bank(O3_BANK, g), lambda k, b: adj_t[:, g, k, half(b)],
                            lambda k: s3[:, g, k, :], S["o3_ps"])
            pairs(pe, pair_of_graphs)
            prefix(PAIRS - 1)
            pe.wait_ge(S["run_made"], PAIRS)
            nc.tensor.matmul(COUNTS, ones_b[:, :], run_cnt[:, :], start=True, stop=True).then_inc(S["total_ps"], 1)
            pe.wait_ge(S["count_made"], 1)

            def rows_in(j, u):
                i = U * j + u
                n = rows_of(pe, j, u)
                pe.wait_ge(xr_loaded[u], 32 * (j + 1))
                if not (is_first(j) and u == 0):
                    pe.wait_ge(S["xt_sb"], i)

                def body(w):
                    for c, m in blocks(w):
                        for k in range(KD):
                            last = nc.tensor.transpose(XT_BANKS[:, k, c * P:c * P + m], xr[0:m, u, c, half(k)],
                                                       ident[0:m, 0:m])
                    last.then_inc(S["xt_ps"], 1)
                by_width(pe, n, body)

            def up(j, u):
                i = U * j + u
                n = rows_of(pe, j, u)
                pe.wait_ge(w1_loaded[u % 2], 16 * uses(j, u))
                pe.wait_ge(S["xt_sb"], i + 1)

                def body(w):
                    for f in range(JF):
                        if not (is_first(j) and u == 0 and f < H_BANKS):
                            pe.wait_ge(S["hid_sb"], JF * i + f + 1 - H_BANKS)
                        for k in range(KD):
                            last = nc.tensor.matmul(ps[:, H_BANK + f % H_BANKS, 0:w], w1_sb[:, u % 2, k, half(f)],
                                                    xt[:, u % 2, k, 0:w], start=(k == 0), stop=(k == KD - 1))
                        last.then_inc(S["hid_ps"], 1)
                by_width(pe, n, body)

            def down(j, u):
                i = U * j + u
                n = rows_of(pe, j, u)
                pe.wait_ge(w2_loaded[u % 2], 16 * uses(j, u))
                if not (is_first(j) and u == 0):
                    pe.wait_ge(S["y_made"], i)
                pe.wait_ge(S["hid_sb"], JF * (i + 1))

                def body(w):
                    for c, m in blocks(w):
                        for f in range(JF):
                            last = nc.tensor.matmul(y_bank(c, m), h_t[:, u % 2, f, c * P:c * P + m],
                                                    w2_sb[:, u % 2, f, :], start=(f == 0), stop=(f == JF - 1))
                    last.then_inc(S["down_done"], 1)
                by_width(pe, n, body)

            rows_in(0, 0)
            up(0, 0)
            rows_in(0, 1)

            def round_of_products(j):
                for u in range(U):
                    if not (is_last(j, E // U) and u == 3):
                        up(*later(j, u, 1))
                    if not (is_last(j, E // U) and u >= 2):
                        rows_in(*later(j, u, 2))
                    down(j, u)
            rounds(pe, round_of_products)


_INS = ['x', 'adj', 'L0_gnn_W1', 'L0_gnn_b1', 'L0_gnn_W2', 'L0_gnn_b2', 'L0_gnn_W3', 'L0_gnn_b3',
        'L0_ffn_W_hash', 'L0_ffn_W1', 'L0_ffn_b1', 'L0_ffn_W2', 'L0_ffn_b2']
_OUTS = [((32, 256, 256), 'float32')]


def kernel(**inputs):
    import numpy as _np
    import concourse.bacc as _bacc
    from concourse import mybir as _mybir
    from concourse.bass_utils import run_bass_kernel_spmd as _run

    nc = _bacc.Bacc("TRN2", target_bir_lowering=False, num_devices=1)
    arrays, args = {}, []
    for name in _INS:
        a = _np.ascontiguousarray(inputs[name])
        arrays[f"in_{name}_dram"] = a
        args.append(nc.dram_tensor(f"in_{name}_dram", a.shape, _mybir.dt.from_np(a.dtype), kind="ExternalInput").ap())
    for i, (shape, dtype) in enumerate(_OUTS):
        dt = _mybir.dt.from_np(_np.dtype(dtype))
        args.append(nc.dram_tensor(f"out_{i}_dram", shape, dt, kind="ExternalOutput").ap())
    gnn_then_hash_routed_experts(nc, *args)
    r = _run(nc, [arrays], core_ids=[0])
    got = tuple(r.results[0][f"out_{i}_dram"] for i in range(len(_OUTS)))
    return got[0]
```

```python
import concourse.bass as bass
from concourse import mybir
from contextlib import ExitStack


def gnn_then_hash_routed_experts(
    nc: bass.Bass,
    x: bass.AP,
    adj: bass.AP,
    gw1: bass.AP,
    gb1: bass.AP,
    gw2: bass.AP,
    gb2: bass.AP,
    gw3: bass.AP,
    gb3: bass.AP,
    w_hash: bass.AP,
    ew1: bass.AP,
    eb1: bass.AP,
    ew2: bass.AP,
    eb2: bass.AP,
    out: bass.AP,
):
    fp32 = mybir.dt.float32
    fp32r = mybir.dt.float32r
    bf16 = mybir.dt.bfloat16
    i32 = mybir.dt.int32
    ALU = mybir.AluOpType
    ACT = mybir.ActivationFunctionType
    AX = mybir.AxisListType

    P = 128
    B, N, D = x.shape
    E, _, F = ew1.shape
    K = 2
    T = B * N
    CAP = -(-(T * K * 5) // (E * 4))
    EPS = 1e-5
    BUCKET_SCALE = 8.0

    PAIRS = B // 2
    TPP = 2 * N // P
    KD = D // P
    NT = T // P
    JF = F // P
    WIDTHS = [128, 192, 256, CAP]
    PLAIN = 192
    HIDDEN_RING = 4
    FILL = P
    STRIDE = CAP + FILL
    CB = -(-CAP // P)
    SPARE = CB * P
    ROW = D + 4
    ID, WEIGHT = D, D + 1
    DROPPED = float(1 << 20)
    U = 4
    HALF = E // 2
    SENT = 16 * CB

    def blocks(w):
        return [(c, min(P, w - c * P)) for c in range(-(-w // P))]

    rows_hbm = nc.dram_tensor("expert_rows", (E * STRIDE, ROW), fp32, kind="Internal").ap()
    x_tok = x.rearrange("b n d -> (b n) d")
    adj_tok = adj.rearrange("b n m -> (b n) m")

    ctx = ExitStack()
    with ctx:
        def sb(name, shape, dt=fp32):
            return ctx.enter_context(nc.sbuf_tensor(name, shape, dt))

        def sem(name):
            return ctx.enter_context(nc.semaphore(name))

        ident = sb("ident", [P, P])
        eb1_t = sb("eb1_t", [P, JF, E])
        empty_row = sb("empty_row", [FILL, ROW])
        count = sb("count", [P, E], i32)
        spare_no = sb("spare_no", [P, CB])
        with ExitStack() as first:
            def sb1(name, shape, dt=fp32):
                return first.enter_context(nc.sbuf_tensor(name, shape, dt))

            y_t = sb1("y_t", [P, 2, KD, N])
            h1_t = sb1("h1_t", [P, 2, KD, N])
            s2 = sb1("s2", [P, 2, KD, D])
            h2_t = sb1("h2_t", [P, 2, KD, N])
            xn = sb1("xn", [P, TPP, D])
            x_in = sb1("x_in", [P, TPP, D])
            adj_in = sb1("adj_in", [P, TPP, N])
            ones_f = sb1("ones_f", [P, P])
            ones_b = sb1("ones_b", [P, P], bf16)
            before = sb1("before", [P, P], bf16)
            expert_no = sb1("expert_no", [P, E])
            token_no = sb1("token_no", [P, PAIRS, TPP])
            minus_half = sb1("minus_half", [P, TPP])
            gw1_sb = sb1("gw1_sb", [P, KD, D])
            gw2_sb = sb1("gw2_sb", [P, KD, D])
            gw3_sb = sb1("gw3_sb", [P, KD, D])
            gb1_sb = sb1("gb1_sb", [P, KD])
            gb2_sb = sb1("gb2_sb", [P, KD])
            gb3_bc = sb1("gb3_bc", [P, D])
            hash_bc = sb1("hash_bc", [P, K, D])
            eb1_in = sb1("eb1_in", [E, F])
            xb3 = sb1("xb3", [P, TPP, D])
            x1 = sb1("x1", [P, TPP, D])
            adj_t = sb1("adj_t", [P, 2, KD, N])
            s3 = sb1("s3", [P, 2, KD, D])
            stats = sb1("stats", [P, TPP, 6])
            mv = sb1("mv", [P, 2, TPP, 2])
            var_e = sb1("var_e", [P, 2, TPP])
            rstd = sb1("rstd", [P, 2, 4, TPP])
            shift = sb1("shift", [P, TPP])
            payload = sb1("payload", [P, K, TPP, ROW])
            prod = sb1("prod", [P, K * TPP, D])
            score = sb1("score", [P, K * TPP])
            floor_i = sb1("floor_i", [P, 3, K * TPP], i32)
            floor_f = sb1("floor_f", [P, 3, K * TPP])
            bucket = sb1("bucket", [P, K * TPP])
            same = sb1("same", [P, TPP])
            onehot = sb1("onehot", [P, K, TPP, E], bf16)
            tile_cnt = sb1("tile_cnt", [P, TPP, E], bf16)
            two_cnt = sb1("two_cnt", [P, 2, E], bf16)
            run_cnt = sb1("run_cnt", [P, E], bf16)
            picked = sb1("picked", [P, K * TPP * E])
            pos = sb1("pos", [P, 3, K * TPP])
            both = sb1("both", [P, 2, TPP])
            slot = sb1("slot", [P, K * TPP], i32)
        w2_hi = sb("w2_hi", [P, 2, JF, D], fp32r)
        w2_low = sb("w2_low", [P, 2, JF, D], fp32r)
        h_hi = sb("h_hi", [P, JF, CAP], fp32r)
        h_lo = sb("h_lo", [P, JF, CAP], fp32r)
        hid = sb("hid", [P, HIDDEN_RING, CAP])
        xt_hi = sb("xt_hi", [P, 2, KD, CAP], fp32r)
        xt_lo = sb("xt_lo", [P, 2, KD, CAP], fp32r)
        xt = sb("xt", [P, 2, KD, CAP])
        y_bias = sb("y_bias", [P, CB, D])
        y_out = sb("y_out", [P, 2, CB, D])
        row_no = sb("row_no", [P, 2, CB])
        row_i = sb("row_i", [P, U, CB], i32)
        xr = sb("xr", [P, U, CB, ROW])
        eb2_bc = sb("eb2_bc", [P, 2, D])
        w2_half = sb("w2_half", [P, 2, JF // 2, D])
        w1_sb = sb("w1_sb", [P, U, KD, F])
        w1_hi = sb("w1_hi", [P, 2, KD, F], fp32r)
        w1_lo = sb("w1_lo", [P, 2, KD, F], fp32r)

        ps = ctx.enter_context(nc.psum_tensor("ps", [P, 8, 512], fp32))
        T_BANK, Y_BANK, H1_BANK, S2_BANK, H2_BANK, S3_BANK, O3_BANK = 0, 1, 2, 3, 0, 1, 2
        PREFIX = ps[:, 3, 0:TPP * E]
        COUNTS = ps[:, 7, 0:E]
        XT_BANKS, H_BANK, H_BANKS, Y_BANK2 = ps[:, 0:2, :], 2, 4, 6

        def bank(b, g):
            return ps[:, 4 * g + b, :].rearrange("p (k n) -> p k n", k=2)

        def y_bank(c, m):
            return ps[0:m, Y_BANK2 + c // 2, (c % 2) * D:(c % 2) * D + D]

        S = {n: sem(n) for n in """
            adj_loaded x_loaded consts_in eb1_loaded consts_made
            adj_t_ps y_ps h1_ps s2_ps h2_ps s3_ps o3_ps
            adj_t_sb y_sb h1_sb s2_sb h2_sb s3_sb x1_made
            xn_made xb3_made scale_made var_made rough_made cnt_made prefix_ps prefix_read run_made
            slots_made rows_made rows_copied rows_sent x1_stored spare_zeroed rows_known y_bias total_ps count_made b1_ps b1_sb dve_step pool_step
            xt_ps xt_sb hid_ps gelu_done hid_hi hid_lo down_done xt_hi w1_hi w1_lo w2_hi y_made passed""".split()}
        y_sent = [sem(f"y_sent{u}") for u in range(U)]
        filled = [sem(f"filled{u}") for u in range(U)]
        xr_loaded = [sem(f"xr_loaded{u}") for u in range(U)]
        w1_loaded = [sem(f"w1_loaded{u}") for u in range(U)]
        w2_loaded = [sem(f"w2_loaded{h}") for h in range(2)]
        w2_lo = [sem(f"w2_lo{h}") for h in range(2)]
        b2_loaded = [sem(f"b2_loaded{s}") for s in range(2)]
        N_CONSTS = 8

        block = ctx.enter_context(nc.Block())

        def expert(j, u):
            return 2 * j + u // 2 + HALF * (u % 2)

        def later(j, u, d):
            return j + (u + d) // U, (u + d) % U

        def uses(j, u):
            return 2 * j + u // 2 + 1

        def rounds_sent(eng, j, u, d):
            at, place = later(j, u, d)
            eng.wait_ge(y_sent[place], SENT * (at + 1))

        def counts_of(eng, which, j, ahead):
            n = U + (0 if is_last(j, E // U) else ahead)
            return nc.values_load_multi_w_load_instructions(
                count[0:1, bass.ds(U * j, n)], engines=(which,), min_val=0, max_val=CAP)[1]

        def by_width(eng, n, body):
            with eng.If(n < WIDTHS[0] + 1):
                body(WIDTHS[0])
            with eng.Else():
                with eng.If(n < WIDTHS[2] + 1):
                    with eng.If(n < WIDTHS[1] + 1):
                        body(WIDTHS[1])
                    with eng.Else():
                        body(WIDTHS[2])
                with eng.Else():
                    body(WIDTHS[3])

        def rounds(eng, body):
            body(0)
            with eng.Fori(1, E // U - 1) as j:
                body(j)
            body(E // U - 1)

        def pairs(eng, body):
            body(0)
            with eng.Fori(1, PAIRS - 1) as i:
                body(i)
            body(PAIRS - 1)

        def passed(eng):
            eng.sem_inc(S["passed"], 1)

        def is_first(i):
            return isinstance(i, int) and i == 0

        def is_last(i, n):
            return isinstance(i, int) and i == n - 1

        @block.sync
        def _(sp):
            def load_x(i):
                sp.dma_start(x_in[:, :, :], x_tok[bass.ds(i * 2 * N, 2 * N), :].rearrange(
                    "(t p) d -> p t d", p=P)).then_inc(S["x_loaded"], 16)

            def load_adj(i):
                sp.dma_start(adj_in[:, :, :], adj_tok[bass.ds(i * 2 * N, 2 * N), :].rearrange(
                    "(t p) d -> p t d", p=P)).then_inc(S["adj_loaded"], 16)

            def store_x1(i):
                sp.wait_ge(S["x1_made"], 2 * i + 2)
                sp.dma_start(out[bass.ds(i * 2 * N, 2 * N), :].rearrange("(t p) d -> p t d", p=P),
                             x1[:, :, :]).then_inc(S["x1_stored"], 16)

            def load_w1(j, u):
                sp.dma_start(w1_sb[:, u, :, :], ew1[expert(j, u)].rearrange(
                    "(k p) f -> p k f", p=P)).then_inc(w1_loaded[u], 16)

            def load_w2(j, u, h):
                sp.dma_start(w2_half[:, h, :, :], ew2[expert(j, u), h * F // 2:(h + 1) * F // 2, :].rearrange(
                    "(f p) d -> p f d", p=P)).then_inc(w2_loaded[h], 16)

            def load_b2(j, u):
                sp.dma_start(eb2_bc[:, u % 2, :], eb2[expert(j, u), :].partition_broadcast(
                    P)).then_inc(b2_loaded[u % 2], 16)

            load_adj(0)
            load_x(0)
            sp.dma_start(gw1_sb[:, :, :], gw1.rearrange("(k p) d -> p k d", p=P)).then_inc(S["consts_in"], 16)
            with nc.allow_non_contiguous_dma(reason="256 bias values, once"):
                sp.dma_start(gb1_sb[:, :], gb1.rearrange("(k p) -> p k", p=P)).then_inc(S["consts_in"], 16)
                sp.dma_start(gb2_sb[:, :], gb2.rearrange("(k p) -> p k", p=P)).then_inc(S["consts_in"], 16)
            sp.dma_start(gw2_sb[:, :, :], gw2.rearrange("(k p) d -> p k d", p=P)).then_inc(S["consts_in"], 16)
            sp.dma_start(gw3_sb[:, :, :], gw3.rearrange("(k p) d -> p k d", p=P)).then_inc(S["consts_in"], 16)
            sp.dma_start(gb3_bc[:, :], gb3.partition_broadcast(P)).then_inc(S["consts_in"], 16)
            for k in range(K):
                sp.dma_start(hash_bc[:, k, :], w_hash[k, :].partition_broadcast(P)).then_inc(S["consts_in"], 16)
            sp.dma_start(eb1_in[:, :], eb1).then_inc(S["eb1_loaded"], 16)
            sp.wait_ge(S["consts_made"], 1)
            sp.dma_start(out[T:T + SPARE, :].rearrange("(c p) d -> p c d", p=P),
                         xr[:, 0, :, 0:D]).then_inc(S["spare_zeroed"], 16)
            for h in range(2):
                load_w2(0, 0, h)
            for u in range(3):
                load_w1(0, u)
            load_b2(0, 0)
            with sp.Fori(1, PAIRS) as i:
                sp.wait_ge(S["adj_t_ps"], 2 * i)
                load_adj(i)
                sp.wait_ge(S["xn_made"], i)
                sp.wait_ge(S["xb3_made"], i)
                load_x(i)
                store_x1(i - 1)
            store_x1(PAIRS - 1)

            def fill(j, u, n):
                sp.dma_start(rows_hbm[bass.ds(expert(j, u) * STRIDE + n, FILL), :],
                             empty_row[:, :]).then_inc(filled[u], 16)

            def load_rows(j, u, n):
                row = expert(j, u) * STRIDE
                sp.wait_ge(filled[u], 16 * (j + 1))
                passed(sp)

                def body(w):
                    full, rest = w // P, w % P
                    if full:
                        sp.dma_start(xr[:, u, 0:full, :], rows_hbm[bass.ds(row, full * P), :].rearrange(
                            "(c p) d -> p c d", p=P)).then_inc(xr_loaded[u], 16 if rest else 32)
                    if rest:
                        sp.dma_start(xr[0:rest, u, full, :], rows_hbm[bass.ds(
                            row + full * P, rest), :]).then_inc(xr_loaded[u], 16 if full else 32)
                by_width(sp, n, body)

            sp.wait_ge(S["count_made"], 1)
            passed(sp)
            first_counts = counts_of(sp, mybir.EngineType.SP, 0, U)
            for u in range(U):
                fill(0, u, first_counts[u])
            sp.wait_ge(S["spare_zeroed"], 16)
            sp.wait_ge(S["rows_sent"], 16 * K * NT)
            passed(sp)
            for u in range(3):
                load_rows(0, u, first_counts[u])

            def round_of_loads(j):
                n = first_counts if is_first(j) else counts_of(sp, mybir.EngineType.SP, j, U)
                for u in range(U):
                    i = U * j + u
                    if not (is_last(j, E // U) and u == 3):
                        for h in range(2):
                            sp.wait_ge(w2_lo[h], i + 1)
                            load_w2(*later(j, u, 1), h)
                        if not (is_first(j) and u == 0):
                            sp.wait_ge(S["y_bias"], i)
                        load_b2(*later(j, u, 1))
                    if not is_last(j, E // U):
                        fill(*later(j, u, U), n[u + U])
                    if not (is_last(j, E // U) and u >= 1):
                        if not (is_first(j) and u == 0):
                            sp.wait_ge(S["hid_ps"], JF * i)
                        load_w1(*later(j, u, 3))
                        if not (is_first(j) and u == 0):
                            sp.wait_ge(S["y_made"], i)
                            passed(sp)
                        load_rows(*later(j, u, 3), n[u + 3])
            rounds(sp, round_of_loads)

            for u in range(U):
                sp.wait_ge(y_sent[u], SENT * (E // U))

        @block.gpsimd
        def _(pool):
            nc.gpsimd.memset(xr[:, :, :, :], 0.0)
            nc.gpsimd.memset(ones_f[:, :], 1.0)
            nc.gpsimd.memset(ones_b[:, :], 1.0)
            nc.gpsimd.memset(run_cnt[:, :], 0.0)
            nc.gpsimd.memset(minus_half[:, :], -0.5)
            nc.gpsimd.memset(payload[:, :, :, :], 1.0 / K)
            nc.gpsimd.memset(empty_row[:, :], 0.0).then_inc(S["pool_step"], 1)
            pool.wait_ge(S["pool_step"], 1)
            nc.gpsimd.memset(empty_row[:, ID:ID + 1], float(T))
            nc.gpsimd.affine_select(out=ident[:, :], in_=ones_f[:, :], compare_op=ALU.is_equal, fill=0.0, base=0,
                                    pattern=[[-1, P]], channel_multiplier=1)
            nc.gpsimd.affine_select(out=before[:, :], in_=ones_b[:, :], compare_op=ALU.is_gt, fill=0.0, base=0,
                                    pattern=[[1, P]], channel_multiplier=-1)
            nc.gpsimd.iota(expert_no[:, :], pattern=[[1, E]], base=0, channel_multiplier=0,
                           allow_small_or_imprecise_dtypes=True)
            nc.gpsimd.iota(spare_no[:, :], pattern=[[P, CB]], base=0, channel_multiplier=1,
                           allow_small_or_imprecise_dtypes=True)
            nc.gpsimd.iota(token_no[:, :, :], pattern=[[TPP * P, PAIRS], [P, TPP]], base=0, channel_multiplier=1,
                           allow_small_or_imprecise_dtypes=True).then_inc(S["consts_made"], 1)
            pool.wait_ge(S["consts_in"], 16 * N_CONSTS)

            def add_b3(i):
                pool.wait_ge(S["x_loaded"], 16 * (i + 1))
                if not is_first(i):
                    pool.wait_ge(S["x1_made"], 2 * i)
                nc.gpsimd.tensor_tensor(xb3[:, :, :], x_in[:, :, :],
                                        gb3_bc[:, :].unsqueeze(1).to_broadcast([P, TPP, D]),
                                        ALU.add).then_inc(S["xb3_made"], 1)

            def count_pair(i):
                pool.wait_ge(S["prefix_ps"], i + 1)
                nc.gpsimd.tensor_tensor(two_cnt[:, :, :], tile_cnt[:, 0:2, :], tile_cnt[:, 2:4, :],
                                        ALU.add).then_inc(S["pool_step"], 1)
                pool.wait_ge(S["pool_step"], 2 * i + 2)
                nc.gpsimd.tensor_tensor(run_cnt[:, :], run_cnt[:, :], two_cnt[:, 0, :], ALU.add).then_inc(S["pool_step"], 1)
                pool.wait_ge(S["pool_step"], 2 * i + 3)
                nc.gpsimd.tensor_tensor(run_cnt[:, :], run_cnt[:, :], two_cnt[:, 1, :], ALU.add).then_inc(S["run_made"], 1)
                pool.wait_ge(S["run_made"], i + 1)

            def send_rows(i):
                pool.wait_ge(S["rows_copied"], i + 1)
                pool.wait_ge(S["slots_made"], i + 1)
                passed(pool)
                for k in range(K):
                    for t in range(TPP):
                        c = k * TPP + t
                        nc.gpsimd.indirect_dma_start(
                            out=rows_hbm, out_offset=bass.IndirectOffsetOnAxis(ap=slot[:, c:c + 1], axis=0),
                            in_=payload[:, k, t, :], in_offset=None, bounds_check=E * STRIDE - 1,
                            oob_is_err=False).then_inc(S["rows_sent"], 16)

            def rough_rstd(which, n):
                pool.wait_ge(S["var_made"], n)
                nc.gpsimd.tensor_tensor(rstd[:, which, 0, :], var_e[:, which, :], minus_half[:, :],
                                        ALU.pow).then_inc(S["rough_made"], 1)

            rough_rstd(0, 1)

            def pair_of_graphs(i):
                if not is_first(i):
                    rough_rstd(1, 2 * i + 1)
                add_b3(i)
                if not is_last(i, PAIRS):
                    rough_rstd(0, 2 * i + 2)
                if not is_first(i):
                    count_pair(i - 1)
                    send_rows(i - 1)
            pairs(pool, pair_of_graphs)
            rough_rstd(1, 2 * PAIRS)

            def w1_lo_parts(j, u):
                for q in range(4):
                    pool.wait_ge(S["w1_hi"], 2 * (U * j + u) + q // 2 + 1)
                    cols = slice(q * F // 4, (q + 1) * F // 4)
                    nc.gpsimd.tensor_tensor(w1_lo[:, u % 2, :, cols], w1_sb[:, u, :, cols],
                                            w1_hi[:, u % 2, :, cols].bitcast(fp32), ALU.subtract).then_inc(S["w1_lo"], 1)

            def w2_lo_half(j, u):
                pool.wait_ge(S["w2_hi"], 2 * (U * j + u) + 2)
                nc.gpsimd.tensor_tensor(w2_low[:, u % 2, JF // 2:, :], w2_half[:, 1, :, :],
                                        w2_hi[:, u % 2, JF // 2:, :].bitcast(fp32), ALU.subtract).then_inc(w2_lo[1], 1)

            w1_lo_parts(0, 0)
            w2_lo_half(0, 0)
            count_pair(PAIRS - 1)
            send_rows(PAIRS - 1)

            pool.wait_ge(S["x1_stored"], 16 * PAIRS)
            pool.wait_ge(S["spare_zeroed"], 16)
            pool.wait_ge(S["count_made"], 1)
            passed(pool)

            def send_results(j, u, n):
                def body(w):
                    if not (is_first(j) and u == 0):
                        rounds_sent(pool, j, u, -1)
                    pool.wait_ge(S["y_made"], U * j + u + 1)
                    passed(pool)
                    cs = blocks(w)
                    for c, m in cs:
                        nc.gpsimd.indirect_dma_start(
                            out=out, out_offset=bass.IndirectOffsetOnAxis(ap=row_i[0:m, u, c:c + 1], axis=0),
                            in_=y_out[0:m, u % 2, c, :], in_offset=None, bounds_check=T + SPARE - 1,
                            compute_op=ALU.add).then_inc(y_sent[u], SENT - 16 * (len(cs) - 1) if c == 0 else 16)
                by_width(pool, n, body)

            def w1_lo_where_split(j, u, n):
                with pool.If(n > PLAIN):
                    w1_lo_parts(j, u)
                with pool.Else():
                    pool.wait_ge(S["w1_hi"], 2 * (U * j + u) + 2)
                    passed(pool)
                    for q in range(4):
                        pool.drain().then_inc(S["w1_lo"], 1)

            first_counts = counts_of(pool, mybir.EngineType.Pool, 0, 2)
            w1_lo_where_split(0, 1, first_counts[1])

            def round_of_sends(j):
                n = first_counts if is_first(j) else counts_of(pool, mybir.EngineType.Pool, j, 2)
                for u in range(U):
                    if not (is_last(j, E // U) and u == 3):
                        w2_lo_half(*later(j, u, 1))
                    if not (is_last(j, E // U) and u >= 2):
                        w1_lo_where_split(*later(j, u, 2), n[u + 2])
                    send_results(j, u, n[u])
            rounds(pool, round_of_sends)

        @block.scalar
        def _(act):
            act.wait_ge(S["consts_in"], 16 * N_CONSTS)

            def out_of_psum(to, frm, ready, done, g_no):
                act.wait_ge(ready, g_no + 1)
                nc.scalar.copy(to, frm).then_inc(done, 1)

            def relu_out(to, g, b, bias, ready, done, g_no):
                act.wait_ge(ready, g_no + 1)
                for hb in range(KD):
                    last = nc.scalar.activation(to[:, g, hb, :], bank(b, g)[:, hb, :], ACT.Relu,
                                                bias=bias[:, hb:hb + 1])
                last.then_inc(done, 1)

            act.wait_ge(S["b1_ps"], 1)
            nc.scalar.copy(eb1_t[:, :, :].rearrange("p f e -> p (f e)"), ps[:, 3, :]).then_inc(S["b1_sb"], 1)

            def normalise(i):
                act.wait_ge(S["scale_made"], i + 1)
                for t in range(TPP):
                    last = nc.scalar.activation(xn[:, t, :], x_in[:, t, :], ACT.Identity,
                                                scale=rstd[:, 0, 3, t:t + 1], bias=shift[:, t:t + 1])
                last.then_inc(S["xn_made"], 1)

            normalise(0)

            def pair_of_graphs(i):
                for g in range(2):
                    if not is_first(i):
                        act.wait_ge(S["o3_ps"], 2 * (i - 1) + g + 1)
                    out_of_psum(adj_t[:, g, :, :], bank(T_BANK, g), S["adj_t_ps"], S["adj_t_sb"], 2 * i + g)
                for g in range(2):
                    out_of_psum(y_t[:, g, :, :], bank(Y_BANK, g), S["y_ps"], S["y_sb"], 2 * i + g)
                for g in range(2):
                    relu_out(h1_t, g, H1_BANK, gb1_sb, S["h1_ps"], S["h1_sb"], 2 * i + g)
                for g in range(2):
                    out_of_psum(s2[:, g, :, :], bank(S2_BANK, g), S["s2_ps"], S["s2_sb"], 2 * i + g)
                for g in range(2):
                    relu_out(h2_t, g, H2_BANK, gb2_sb, S["h2_ps"], S["h2_sb"], 2 * i + g)
                if not is_first(i):
                    act.wait_ge(S["rows_made"], i)
                    nc.scalar.copy(payload[:, 1, :, 0:D], payload[:, 0, :, 0:D]).then_inc(S["rows_copied"], 1)
                for g in range(2):
                    out_of_psum(s3[:, g, :, :], bank(S3_BANK, g), S["s3_ps"], S["s3_sb"], 2 * i + g)
                if not is_last(i, PAIRS):
                    normalise(i + 1)
            pairs(act, pair_of_graphs)

            def w2_hi_parts(j, u):
                i = U * j + u
                if not (is_first(j) and u < 2):
                    act.wait_ge(S["down_done"], i - 1)
                for h in range(2):
                    act.wait_ge(w2_loaded[h], 16 * (i + 1))
                    nc.scalar.copy(w2_hi[:, u % 2, h * JF // 2:(h + 1) * JF // 2, :],
                                   w2_half[:, h, :, :]).then_inc(S["w2_hi"], 1)

            act.wait_ge(w1_loaded[0], 16)
            for h in range(2):
                cols = slice(h * F // 2, (h + 1) * F // 2)
                nc.scalar.copy(w1_hi[:, 0, :, cols], w1_sb[:, 0, :, cols]).then_inc(S["w1_hi"], 1)
            w2_hi_parts(0, 0)
            act.wait_ge(S["rows_made"], PAIRS)
            nc.scalar.copy(payload[:, 1, :, 0:D], payload[:, 0, :, 0:D]).then_inc(S["rows_copied"], 1)

            act.wait_ge(S["count_made"], 1)
            act.wait_ge(S["b1_sb"], 1)
            passed(act)

            def round_of_gelus(j):
                n = counts_of(act, mybir.EngineType.Activation, j, 0)
                for u in range(U):
                    i = U * j + u
                    bias = bass.ds(expert(j, u), 1)

                    def body(w):
                        for f in range(JF):
                            if f == 0 and w > PLAIN and not (is_first(j) and u == 0):
                                act.wait_ge(S["down_done"], i)
                            act.wait_ge(S["hid_ps"], JF * i + f + 1)
                            if not (is_first(j) and u == 0 and f < HIDDEN_RING):
                                act.wait_ge(S["hid_lo"], JF // 2 * i + (f - HIDDEN_RING) // 2 + 1)
                            h_ps = ps[:, H_BANK + f % H_BANKS, 0:w]
                            last = nc.scalar.activation(hid[:, f % HIDDEN_RING, 0:w], h_ps, ACT.Gelu,
                                                        bias=eb1_t[:, f, bias])
                            if w > PLAIN:
                                last = nc.scalar.activation(h_hi[:, f, 0:w], h_ps, ACT.Gelu, bias=eb1_t[:, f, bias])
                            last.then_inc(S["gelu_done"], 1)
                        act.wait_ge(b2_loaded[u % 2], 16 * uses(j, u))
                        if not (is_first(j) and u == 0):
                            act.wait_ge(S["y_made"], i)
                        for c, m in blocks(P if w <= P else CAP):
                            last = nc.scalar.activation(y_bias[0:m, c, :], eb2_bc[0:m, u % 2, :], ACT.Copy,
                                                        scale=xr[0:m, u, c, WEIGHT:WEIGHT + 1])
                        last.then_inc(S["y_bias"], 1)
                    by_width(act, n[u], body)
                    if not (is_last(j, E // U) and u == 3):
                        w2_hi_parts(*later(j, u, 1))
            rounds(act, round_of_gelus)

        @block.vector
        def _(dve):
            PER_PAIR = 6 + 4 + 16
            made = {"base": 0, "n": 0}

            def step(ins):
                made["n"] += 1
                ins.then_inc(S["dve_step"], 1)
                dve.wait_ge(S["dve_step"], made["base"] + made["n"])

            def variances(which, src):
                for t in range(TPP):
                    last = nc.vector.bn_stats(stats[:, t, :], src(t))
                step(last)
                passed(dve)
                for t in range(TPP):
                    last = nc.vector.bn_aggr(mv[:, which, t, :], stats[:, t, :])
                step(last)
                nc.vector.tensor_scalar(var_e[:, which, :], mv[:, which, :, 1], EPS, None,
                                        ALU.add).then_inc(S["var_made"], 1)

            def scales(which, n_norm):
                r = rstd[:, which, :, :]
                dve.wait_ge(S["rough_made"], n_norm)
                step(nc.vector.tensor_tensor(r[:, 1, :], r[:, 0, :], r[:, 0, :], ALU.mult))
                step(nc.vector.tensor_tensor(r[:, 2, :], r[:, 1, :], var_e[:, which, :], ALU.mult))
                step(nc.vector.tensor_scalar(r[:, 1, :], r[:, 2, :], -0.5, 1.5, ALU.mult, ALU.add))
                step(nc.vector.tensor_tensor(r[:, 3, :], r[:, 0, :], r[:, 1, :], ALU.mult))

            def first_variances(i):
                dve.wait_ge(S["x_loaded"], 16 * (i + 1))
                if not is_first(i):
                    dve.wait_ge(S["xn_made"], i)
                variances(0, lambda t: x_in[:, t, :])

            def first_scales(i, n_norm):
                scales(0, n_norm)
                nc.vector.scalar_tensor_tensor(out=shift[:, :], in0=mv[:, 0, :, 0], scalar=-1.0,
                                               in1=rstd[:, 0, 3, :], op0=ALU.mult,
                                               op1=ALU.mult).then_inc(S["scale_made"], 1)

            def residual(i):
                dve.wait_ge(S["xb3_made"], i + 1)
                if not is_first(i):
                    dve.wait_ge(S["x1_stored"], 16 * i)
                for g in range(2):
                    dve.wait_ge(S["o3_ps"], 2 * i + g + 1)
                    nc.vector.tensor_tensor(x1[:, 2 * g:2 * g + 2, :], bank(O3_BANK, g),
                                            xb3[:, 2 * g:2 * g + 2, :], ALU.add).then_inc(S["x1_made"], 1)
                dve.wait_ge(S["x1_made"], 2 * i + 2)
                passed(dve)

            def second_norm(i):
                variances(1, lambda t: x1[:, t, :])
                scales(1, 2 * i + 3 if not is_last(i, PAIRS) else 2 * PAIRS)
                if not is_first(i):
                    dve.wait_ge(S["rows_sent"], 16 * K * TPP * i)
                for t in range(TPP):
                    last = nc.vector.tensor_scalar(payload[:, 0, t, 0:D], x1[:, t, :], mv[:, 1, t, 0:1],
                                                   rstd[:, 1, 3, t:t + 1], ALU.subtract, ALU.mult)
                last.then_inc(S["rows_made"], 1)
                dve.wait_ge(S["rows_made"], i + 1)
                for k in range(K):
                    for t in range(TPP):
                        c = k * TPP + t
                        last = nc.vector.tensor_tensor_reduce(
                            out=prod[:, c, :], in0=payload[:, 0, t, 0:D], in1=hash_bc[:, k, :], scale=1.0,
                            scalar=0.0, op0=ALU.mult, op1=ALU.add, accum_out=score[:, c:c + 1])
                step(last)
                step(nc.vector.tensor_scalar(floor_i[:, 0, :], score[:, :], BUCKET_SCALE, None, ALU.mult))
                step(nc.vector.tensor_copy(floor_f[:, 0, :], floor_i[:, 0, :]))
                step(nc.vector.scalar_tensor_tensor(out=floor_f[:, 1, :], in0=score[:, :], scalar=BUCKET_SCALE,
                                                    in1=floor_f[:, 0, :], op0=ALU.mult, op1=ALU.is_lt))
                step(nc.vector.tensor_tensor(floor_f[:, 2, :], floor_f[:, 0, :], floor_f[:, 1, :], ALU.subtract))
                step(nc.vector.tensor_copy(floor_i[:, 1, :], floor_f[:, 2, :]))
                step(nc.vector.tensor_scalar(floor_i[:, 2, :], floor_i[:, 1, :], E - 1, None, ALU.bitwise_and))
                step(nc.vector.tensor_copy(bucket[:, :], floor_i[:, 2, :]))
                step(nc.vector.tensor_tensor(same[:, :], bucket[:, 0:TPP], bucket[:, TPP:2 * TPP], ALU.is_equal))
                step(nc.vector.tensor_tensor(
                    onehot[:, :, :, :].rearrange("p k t e -> p (k t) e"),
                    bucket[:, :].unsqueeze(2).to_broadcast([P, K * TPP, E]),
                    expert_no[:, :].unsqueeze(1).to_broadcast([P, K * TPP, E]), ALU.is_equal))
                if not is_first(i):
                    dve.wait_ge(S["run_made"], i)
                nc.vector.tensor_tensor(tile_cnt[:, :, :], onehot[:, 0, :, :], onehot[:, 1, :, :],
                                        ALU.add).then_inc(S["cnt_made"], 1)

            def slots(i):
                dve.wait_ge(S["prefix_ps"], i + 1)
                if not is_first(i):
                    dve.wait_ge(S["rows_sent"], 16 * K * TPP * i)
                nc.vector.tensor_tensor(
                    picked[:, :].rearrange("p (k c) -> p k c", k=K),
                    onehot[:, :, :, :].rearrange("p k t e -> p k (t e)"),
                    PREFIX.unsqueeze(1).to_broadcast([P, K, TPP * E]), ALU.mult).then_inc(S["prefix_read"], 1)
                dve.wait_ge(S["prefix_read"], i + 2)
                step(nc.vector.tensor_reduce(pos[:, 0, :], picked[:, :].rearrange("p (c e) -> p c e", e=E), AX.X, ALU.add))
                step(nc.vector.tensor_tensor(pos[:, 0, TPP:2 * TPP], pos[:, 0, TPP:2 * TPP], same[:, :], ALU.add))
                nc.vector.scalar_tensor_tensor(out=pos[:, 1, :], in0=bucket[:, :], scalar=float(STRIDE),
                                               in1=pos[:, 0, :], op0=ALU.mult, op1=ALU.add)
                nc.vector.tensor_scalar(pos[:, 2, :], pos[:, 0, :], float(CAP), DROPPED, ALU.is_ge, ALU.mult)
                step(nc.vector.scalar_tensor_tensor(out=both[:, 0, :], in0=pos[:, 0, TPP:2 * TPP], scalar=float(CAP),
                                                    in1=same[:, :], op0=ALU.is_lt, op1=ALU.mult))
                nc.vector.tensor_scalar(both[:, 1, :], same[:, :], float(T), None, ALU.mult)
                number = token_no[:, bass.ds(i, 1), :].rearrange("p o t -> p (o t)")
                nc.vector.tensor_scalar(payload[:, 0, :, WEIGHT], both[:, 0, :], 1.0 / K, 1.0 / K, ALU.mult, ALU.add)
                nc.vector.tensor_copy(payload[:, 0, :, ID], number)
                step(nc.vector.tensor_tensor(slot[:, :], pos[:, 1, :], pos[:, 2, :], ALU.add))
                nc.vector.tensor_tensor(payload[:, 1, :, ID], both[:, 1, :], number,
                                        ALU.max).then_inc(S["slots_made"], 1)
                dve.wait_ge(S["slots_made"], i + 1)

            dve.sem_inc(S["prefix_read"], 1)
            first_variances(0)
            first_scales(0, 1)

            def pair_of_graphs(i):
                at = made["n"]
                if not isinstance(i, int):
                    made["base"] = (i - 1) * PER_PAIR
                if not is_last(i, PAIRS):
                    first_variances(i + 1)
                if not is_first(i):
                    slots(i - 1)
                if not is_last(i, PAIRS):
                    first_scales(i + 1, 2 * i + 2)
                residual(i)
                second_norm(i)
                if not isinstance(i, int):
                    assert made["n"] - at == PER_PAIR, (made["n"] - at, PER_PAIR)
                    made["base"], made["n"] = 0, made["n"] + (PAIRS - 3) * PER_PAIR
            pairs(dve, pair_of_graphs)
            slots(PAIRS - 1)

            dve.wait_ge(S["total_ps"], 1)
            nc.vector.tensor_scalar(count[:, :].rearrange("p (a h) -> p h a", h=2),
                                    COUNTS.rearrange("p (h a) -> p h a", h=2), float(CAP), None,
                                    ALU.min).then_inc(S["count_made"], 1)
            dve.wait_ge(S["count_made"], 1)
            passed(dve)

            def hidden_parts(j, u, n):
                i = U * j + u

                def body(w):
                    for g in range(JF // 2):
                        fs = slice(2 * g, 2 * g + 2)
                        ring = hid[:, 2 * g % HIDDEN_RING:2 * g % HIDDEN_RING + 2, 0:w]
                        if g == 0 and w <= PLAIN and not (is_first(j) and u == 0):
                            dve.wait_ge(S["down_done"], i)
                        dve.wait_ge(S["gelu_done"], JF * i + 2 * g + 2)
                        if w <= PLAIN:
                            nc.vector.tensor_copy(h_hi[:, fs, 0:w], ring).then_inc(S["hid_hi"], 1)
                        else:
                            dve.sem_inc(S["hid_hi"], 1)
                        dve.wait_ge(S["hid_hi"], JF // 2 * i + g + 1)
                        nc.vector.tensor_tensor(h_lo[:, fs, 0:w], ring, h_hi[:, fs, 0:w].bitcast(fp32),
                                                ALU.subtract).then_inc(S["hid_lo"], 1)
                by_width(dve, n, body)

            def rows_out(j, u, n):
                i = U * j + u

                def body(w):
                    if not (is_first(j) and u < 2):
                        dve.wait_ge(S["hid_ps"], JF * (i - 1))
                    dve.wait_ge(S["xt_ps"], i + 1)
                    if w > PLAIN:
                        nc.vector.tensor_copy(xt_hi[:, u % 2, :, 0:w], XT_BANKS[:, :, 0:w]).then_inc(S["xt_hi"], 1)
                        dve.wait_ge(S["xt_hi"], i + 1)
                        nc.vector.tensor_tensor(xt_lo[:, u % 2, :, 0:w], XT_BANKS[:, :, 0:w],
                                                xt_hi[:, u % 2, :, 0:w].bitcast(fp32),
                                                ALU.subtract).then_inc(S["xt_sb"], 1)
                    else:
                        for k, done in enumerate((S["xt_hi"], S["xt_sb"])):
                            nc.vector.tensor_copy(xt[:, u % 2, k, 0:w], XT_BANKS[:, k, 0:w]).then_inc(done, 1)
                by_width(dve, n, body)

            def w1_hi_parts(j, u, n):
                with dve.If(n > PLAIN):
                    dve.wait_ge(w1_loaded[u], 16 * (j + 1))
                    for h in range(2):
                        cols = slice(h * F // 2, (h + 1) * F // 2)
                        nc.vector.tensor_copy(w1_hi[:, u % 2, :, cols], w1_sb[:, u, :, cols]).then_inc(S["w1_hi"], 1)
                with dve.Else():
                    for h in range(2):
                        dve.drain().then_inc(S["w1_hi"], 1)

            def w2_lo_half(j, u):
                dve.wait_ge(S["w2_hi"], 2 * (U * j + u) + 1)
                nc.vector.tensor_tensor(w2_low[:, u % 2, 0:JF // 2, :], w2_half[:, 0, :, :],
                                        w2_hi[:, u % 2, 0:JF // 2, :].bitcast(fp32), ALU.subtract).then_inc(w2_lo[0], 1)

            def results_out(j, u, n):
                i = U * j + u
                ids = xr[:, u, :, ID:ID + 1].rearrange("p c o -> p (c o)")
                dve.wait_ge(S["xt_ps"], i + 1)
                nc.vector.scalar_tensor_tensor(out=row_no[:, u % 2, :], in0=ids, scalar=float(T),
                                               in1=spare_no[:, :], op0=ALU.is_ge, op1=ALU.mult).then_inc(S["rows_known"], 1)
                if not (is_first(j) and u < 2):
                    rounds_sent(dve, j, u, -2)
                dve.wait_ge(S["rows_known"], i + 1)
                nc.vector.tensor_tensor(row_i[:, u, :], row_no[:, u % 2, :], ids, ALU.add)

                def weigh(c, m):
                    return nc.vector.scalar_tensor_tensor(
                        out=y_out[0:m, u % 2, c, :], in0=y_bank(c, m), scalar=xr[0:m, u, c, WEIGHT:WEIGHT + 1],
                        in1=y_bias[0:m, c, :], op0=ALU.mult, op1=ALU.add)

                def body(rows):
                    dve.wait_ge(S["y_bias"], i + 1)
                    dve.wait_ge(S["down_done"], i + 1)
                    for c, m in blocks(rows):
                        last = weigh(c, m)
                    last.then_inc(S["y_made"], 1)

                with dve.If(n < P + 1):
                    body(P)
                with dve.Else():
                    body(CAP)

            def one_count(j, u):
                return nc.values_load_multi_w_load_instructions(
                    count[0:1, bass.ds(U * j + u, 1)], engines=(mybir.EngineType.DVE,), min_val=0, max_val=CAP)[1][0]

            w2_lo_half(0, 0)
            first_counts = [one_count(0, 0), one_count(0, 1)]
            rows_out(0, 0, first_counts[0])
            rows_out(0, 1, first_counts[1])
            w1_hi_parts(0, 1, first_counts[1])

            def round_of_results(j):
                n = list(first_counts) if is_first(j) else [one_count(j, 0), one_count(j, 1)]
                for u in range(U):
                    hidden_parts(j, u, n[u])
                    if not (is_last(j, E // U) and u >= 2):
                        n.append(one_count(j, u + 2))
                        rows_out(*later(j, u, 2), n[u + 2])
                        w1_hi_parts(*later(j, u, 2), n[u + 2])
                    if not (is_last(j, E // U) and u == 3):
                        w2_lo_half(*later(j, u, 1))
                    results_out(j, u, n[u])
            rounds(dve, round_of_results)

        @block.tensor
        def _(pe):
            pe.wait_ge(S["consts_made"], 1)
            pe.wait_ge(S["consts_in"], 16 * N_CONSTS)
            pe.wait_ge(S["eb1_loaded"], 16)

            def product(to, lhs, rhs, done):
                for b in range(KD):
                    for k in range(KD):
                        last = nc.tensor.matmul(to[:, b, :], lhs(k, b), rhs(k), start=(k == 0), stop=(k == KD - 1))
                last.then_inc(done, 1)

            def half(b):
                return slice(b * P, b * P + P)

            for f in range(JF):
                last = nc.tensor.transpose(ps[:, 3, f * E:f * E + E], eb1_in[:, f * P:f * P + P], ident[0:E, 0:E])
            last.then_inc(S["b1_ps"], 1)

            def prefix(i):
                pe.wait_ge(S["cnt_made"], i + 1)
                if not is_first(i):
                    pe.wait_ge(S["run_made"], i)
                nc.tensor.matmul(PREFIX, before[:, :], tile_cnt[:, :, :].rearrange("p t e -> p (t e)"),
                                 start=True, stop=False)
                for t in range(TPP - 1):
                    nc.tensor.matmul(PREFIX[:, (t + 1) * E:], ones_b[:, :],
                                     tile_cnt[:, t, :].unsqueeze(1).to_broadcast([P, TPP - 1 - t, E]),
                                     start=False, stop=False)
                nc.tensor.matmul(PREFIX, ones_b[:, :], run_cnt[:, :].unsqueeze(1).to_broadcast([P, TPP, E]),
                                 start=False, stop=True).then_inc(S["prefix_ps"], 1)

            def pair_of_graphs(i):
                for g in range(2):
                    if g == 0:
                        pe.wait_ge(S["adj_loaded"], 16 * (i + 1))
                    for mb in range(KD):
                        for nb in range(KD):
                            last = nc.tensor.transpose(bank(T_BANK, g)[:, mb, half(nb)],
                                                       adj_in[:, 2 * g + nb, half(mb)], ident[:, :])
                    last.then_inc(S["adj_t_ps"], 1)
                for g in range(2):
                    pe.wait_ge(S["xn_made"], i + 1)
                    pe.wait_ge(S["adj_t_sb"], 2 * i + g + 1)
                    product(bank(Y_BANK, g), lambda k, b: xn[:, 2 * g + k, half(b)],
                            lambda k: adj_t[:, g, k, :], S["y_ps"])
                for g in range(2):
                    pe.wait_ge(S["y_sb"], 2 * i + g + 1)
                    if not is_first(i):
                        pe.wait_ge(S["x1_made"], 2 * (i - 1) + g + 1)
                    product(bank(H1_BANK, g), lambda k, b: gw1_sb[:, k, half(b)],
                            lambda k: y_t[:, g, k, :], S["h1_ps"])
                for g in range(2):
                    pe.wait_ge(S["h1_sb"], 2 * i + g + 1)
                    if is_first(i):
                        pe.wait_ge(S["b1_sb"], 1)
                    elif g == 0:
                        pe.wait_ge(S["prefix_read"], i)
                    product(bank(S2_BANK, g), lambda k, b: h1_t[:, g, k, half(b)],
                            lambda k: gw2_sb[:, k, :], S["s2_ps"])
                for g in range(2):
                    pe.wait_ge(S["s2_sb"], 2 * i + g + 1)
                    product(bank(H2_BANK, g), lambda k, b: s2[:, g, k, half(b)],
                            lambda k: adj_t[:, g, k, :], S["h2_ps"])
                if not is_first(i):
                    prefix(i - 1)
                for g in range(2):
                    pe.wait_ge(S["h2_sb"], 2 * i + g + 1)
                    product(bank(S3_BANK, g), lambda k, b: h2_t[:, g, k, half(b)],
                            lambda k: gw3_sb[:, k, :], S["s3_ps"])
                for g in range(2):
                    pe.wait_ge(S["s3_sb"], 2 * i + g + 1)
                    product(bank(O3_BANK, g), lambda k, b: adj_t[:, g, k, half(b)],
                            lambda k: s3[:, g, k, :], S["o3_ps"])
            pairs(pe, pair_of_graphs)
            prefix(PAIRS - 1)
            pe.wait_ge(S["run_made"], PAIRS)
            nc.tensor.matmul(COUNTS, ones_b[:, :], run_cnt[:, :], start=True, stop=True).then_inc(S["total_ps"], 1)
            pe.wait_ge(S["count_made"], 1)
            passed(pe)

            def rows_in(j, u):
                pe.wait_ge(xr_loaded[u], 32 * (j + 1))
                if not (is_first(j) and u == 0):
                    pe.wait_ge(S["xt_sb"], U * j + u)
                for c, m in blocks(CAP):
                    for k in range(KD):
                        last = nc.tensor.transpose(XT_BANKS[:, k, c * P:c * P + m], xr[0:m, u, c, half(k)],
                                                   ident[0:m, 0:m])
                last.then_inc(S["xt_ps"], 1)

            def up(j, u, w):
                i = U * j + u
                pe.wait_ge(w1_loaded[u], 16 * (j + 1))
                pe.wait_ge(S["xt_sb"], i + 1)
                for f in range(JF):
                    if w > PLAIN:
                        pe.wait_ge(S["w1_lo"], 4 * i + f // 2 + 1)
                    if not (is_first(j) and u == 0 and f < H_BANKS):
                        pe.wait_ge(S["gelu_done"], JF * i + f + 1 - H_BANKS)
                    to = ps[:, H_BANK + f % H_BANKS, 0:w]
                    if w > PLAIN:
                        parts = [(wp[:, u % 2, k, half(f)], xp[:, u % 2, k, 0:w]) for k in range(KD)
                                 for wp, xp in ((w1_hi, xt_hi), (w1_hi, xt_lo), (w1_lo, xt_hi))]
                    else:
                        parts = [(w1_sb[:, u, k, half(f)], xt[:, u % 2, k, 0:w]) for k in range(KD)]
                    for at, (lhs, rhs) in enumerate(parts):
                        last = nc.tensor.matmul(to, lhs, rhs, start=(at == 0), stop=(at == len(parts) - 1))
                    last.then_inc(S["hid_ps"], 1)

            def down(j, u, w):
                i = U * j + u
                if not (is_first(j) and u == 0):
                    pe.wait_ge(S["y_made"], i)
                for c, m in blocks(w):
                    for f in range(JF):
                        if c == 0 and f % (JF // 2) == 0:
                            pe.wait_ge(w2_lo[f // (JF // 2)], i + 1)
                        if c == 0 and f % 2 == 0:
                            pe.wait_ge(S["hid_lo"], JF // 2 * i + f // 2 + 1)
                        for at, (hp, wp) in enumerate(((h_hi, w2_hi), (h_hi, w2_low), (h_lo, w2_hi))):
                            last = nc.tensor.matmul(y_bank(c, m), hp[:, f, c * P:c * P + m],
                                                    wp[:, u % 2, f, :], start=(f == 0 and at == 0),
                                                    stop=(f == JF - 1 and at == 2))
                last.then_inc(S["down_done"], 1)

            rows_in(0, 0)
            rows_in(0, 1)

            def round_of_products(j):
                n = counts_of(pe, mybir.EngineType.PE, j, 0)
                for u in range(U):
                    def body(w):
                        up(j, u, w)
                        if not (is_last(j, E // U) and u >= 2):
                            rows_in(*later(j, u, 2))
                        down(j, u, w)
                    by_width(pe, n[u], body)
            rounds(pe, round_of_products)


_INS = ['x', 'adj', 'L0_gnn_W1', 'L0_gnn_b1', 'L0_gnn_W2', 'L0_gnn_b2', 'L0_gnn_W3', 'L0_gnn_b3',
        'L0_ffn_W_hash', 'L0_ffn_W1', 'L0_ffn_b1', 'L0_ffn_W2', 'L0_ffn_b2']
_OUTS = [((32 * 256 + 384, 256), 'float32')]


def kernel(**inputs):
    import numpy as _np
    import concourse.bacc as _bacc
    from concourse import mybir as _mybir
    from concourse.bass_utils import run_bass_kernel_spmd as _run

    nc = _bacc.Bacc("TRN2", target_bir_lowering=False, num_devices=1)
    arrays, args = {}, []
    for name in _INS:
        a = _np.ascontiguousarray(inputs[name])
        arrays[f"in_{name}_dram"] = a
        args.append(nc.dram_tensor(f"in_{name}_dram", a.shape, _mybir.dt.from_np(a.dtype), kind="ExternalInput").ap())
    for i, (shape, dtype) in enumerate(_OUTS):
        dt = _mybir.dt.from_np(_np.dtype(dtype))
        args.append(nc.dram_tensor(f"out_{i}_dram", shape, dt, kind="ExternalOutput").ap())
    gnn_then_hash_routed_experts(nc, *args)
    r = _run(nc, [arrays], core_ids=[0])
    got = tuple(r.results[0][f"out_{i}_dram"] for i in range(len(_OUTS)))
    return got[0][:32 * 256].reshape(32, 256, 256)
```

```python
import concourse.bass as bass
from concourse import mybir
from contextlib import ExitStack


def gnn_then_hash_routed_experts(
    nc: bass.Bass,
    x: bass.AP,
    adj: bass.AP,
    gw1: bass.AP,
    gb1: bass.AP,
    gw2: bass.AP,
    gb2: bass.AP,
    gw3: bass.AP,
    gb3: bass.AP,
    w_hash: bass.AP,
    ew1: bass.AP,
    eb1: bass.AP,
    ew2: bass.AP,
    eb2: bass.AP,
    out: bass.AP,
):
    fp32 = mybir.dt.float32
    fp32r = mybir.dt.float32r
    bf16 = mybir.dt.bfloat16
    i32 = mybir.dt.int32
    ALU = mybir.AluOpType
    ACT = mybir.ActivationFunctionType
    AX = mybir.AxisListType

    P = 128
    B, N, D = x.shape
    E, _, F = ew1.shape
    K = 2
    T = B * N
    CAP = -(-(T * K * 5) // (E * 4))
    EPS = 1e-5
    BUCKET_SCALE = 8.0

    PAIRS = B // 2
    TPP = 2 * N // P
    KD = D // P
    NT = T // P
    JF = F // P
    WIDTHS = [128, 192, 256, CAP]
    PLAIN = 192
    HIDDEN_RING = 4
    FILL = P
    STRIDE = CAP + FILL
    CB = -(-CAP // P)
    SPARE = CB * P
    ROW = D + 4
    ID, WEIGHT = D, D + 1
    DROPPED = float(1 << 20)
    U = 4
    HALF = E // 2
    SENT = 16 * CB

    def blocks(w):
        return [(c, min(P, w - c * P)) for c in range(-(-w // P))]

    rows_hbm = nc.dram_tensor("expert_rows", (E * STRIDE, ROW), fp32, kind="Internal").ap()
    x_tok = x.rearrange("b n d -> (b n) d")
    adj_tok = adj.rearrange("b n m -> (b n) m")

    ctx = ExitStack()
    with ctx:
        def sb(name, shape, dt=fp32):
            return ctx.enter_context(nc.sbuf_tensor(name, shape, dt))

        def sem(name):
            return ctx.enter_context(nc.semaphore(name))

        ident = sb("ident", [P, P])
        eb1_t = sb("eb1_t", [P, JF, E])
        empty_row = sb("empty_row", [FILL, ROW])
        count = sb("count", [P, E], i32)
        width_no = sb("width_no", [P, 3, E])
        widths_of = sb("widths_of", [P, 2, E // U])
        round_widths = sb("round_widths", [P, E // U], i32)
        spare_no = sb("spare_no", [P, CB])
        with ExitStack() as first:
            def sb1(name, shape, dt=fp32):
                return first.enter_context(nc.sbuf_tensor(name, shape, dt))

            y_hi = sb1("y_hi", [P, 2, KD, N], fp32r)
            h1_t = sb1("h1_t", [P, 2, KD, N])
            s2_hi = sb1("s2_hi", [P, 2, KD, D], fp32r)
            h2_t = sb1("h2_t", [P, 2, KD, N])
            xn = sb1("xn", [P, TPP, D])
            x_in = sb1("x_in", [P, TPP, D])
            adj_in = sb1("adj_in", [P, TPP, N])
            ones_f = sb1("ones_f", [P, P])
            ones_b = sb1("ones_b", [P, P], bf16)
            before = sb1("before", [P, P], bf16)
            expert_no = sb1("expert_no", [P, E])
            token_no = sb1("token_no", [P, PAIRS, TPP])
            minus_half = sb1("minus_half", [P, TPP])
            gw1_sb = sb1("gw1_sb", [P, KD, D])
            gw2_sb = sb1("gw2_sb", [P, KD, D])
            gw3_sb = sb1("gw3_sb", [P, KD, D])
            gb1_sb = sb1("gb1_sb", [P, KD])
            gb2_sb = sb1("gb2_sb", [P, KD])
            gb3_bc = sb1("gb3_bc", [P, D])
            hash_bc = sb1("hash_bc", [P, K, D])
            xb3 = sb1("xb3", [P, TPP, D])
            x1 = sb1("x1", [P, TPP, D])
            adj_t = sb1("adj_t", [P, 2, KD, N])
            s3_hi = sb1("s3_hi", [P, 2, KD, D], fp32r)
            y_lo = sb1("y_lo", [P, 2, KD, N], fp32r)
            s2_lo = sb1("s2_lo", [P, 2, KD, D], fp32r)
            s3_lo = sb1("s3_lo", [P, 2, KD, D], fp32r)
            adj_hi = sb1("adj_hi", [P, 2, KD, N], fp32r)
            adj_lo = sb1("adj_lo", [P, 2, KD, N], fp32r)
            gw1_hi = sb1("gw1_hi", [P, KD, D], fp32r)
            gw1_lo = sb1("gw1_lo", [P, KD, D], fp32r)
            stats = sb1("stats", [P, TPP, 6])
            mv = sb1("mv", [P, 2, TPP, 2])
            var_e = sb1("var_e", [P, 2, TPP])
            rstd = sb1("rstd", [P, 2, 4, TPP])
            shift = sb1("shift", [P, TPP])
            rows = sb1("rows", [P, TPP, D])
            payload = sb1("payload", [P, K, TPP, ROW])
            score = sb1("score", [P, K * TPP])
            floor_i = sb1("floor_i", [P, 3, K * TPP], i32)
            floor_f = sb1("floor_f", [P, 3, K * TPP])
            bucket = sb1("bucket", [P, K * TPP])
            same = sb1("same", [P, TPP])
            onehot = sb1("onehot", [P, K, TPP, E], bf16)
            tile_cnt = sb1("tile_cnt", [P, TPP, E], bf16)
            two_cnt = sb1("two_cnt", [P, 2, E], bf16)
            run_cnt = sb1("run_cnt", [P, E], bf16)
            picked = sb1("picked", [P, K * TPP * E])
            pos = sb1("pos", [P, 3, K * TPP])
            both = sb1("both", [P, 2, TPP])
            slot = sb1("slot", [P, K * TPP], i32)
        w2_hi = sb("w2_hi", [P, 2, JF, D], fp32r)
        w2_low = sb("w2_low", [P, 2, JF, D], fp32r)
        h_hi = sb("h_hi", [P, JF, CAP], fp32r)
        h_lo = sb("h_lo", [P, JF, CAP], fp32r)
        hid = sb("hid", [P, HIDDEN_RING, CAP])
        xt_hi = sb("xt_hi", [P, 2, KD, CAP], fp32r)
        xt_lo = sb("xt_lo", [P, 2, KD, CAP], fp32r)
        xt = sb("xt", [P, 2, KD, CAP])
        y_bias = sb("y_bias", [P, CB, D])
        y_out = sb("y_out", [P, 2, CB, D])
        row_no = sb("row_no", [P, 2, CB])
        row_i = sb("row_i", [P, U, CB], i32)
        behind = sb("behind", [P, 14 * D + P])
        xr = sb("xr", [P, U, CB, ROW])
        eb2_bc = sb("eb2_bc", [P, 2, D])
        w2_half = sb("w2_half", [P, 2, JF // 2, D])
        w1_sb = sb("w1_sb", [P, U, KD, F])
        prod = w1_sb[:, U - 1, :, :].rearrange("p k f -> p (k f)").rearrange("p (c d) -> p c d", d=D)
        eb1_in = w1_sb[0:E, U - 1, 0, :]
        w1_hi = sb("w1_hi", [P, 2, KD, F], fp32r)
        w1_lo = sb("w1_lo", [P, 2, KD, F], fp32r)

        ps = ctx.enter_context(nc.psum_tensor("ps", [P, 8, 512], fp32))
        T_BANK, Y_BANK, H1_BANK, S2_BANK, H2_BANK, S3_BANK, O3_BANK = 0, 1, 2, 3, 0, 1, 2
        PREFIX = ps[:, 3, 0:TPP * E]
        COUNTS = ps[:, 7, 0:E]
        XT_BANKS, H_BANK, H_BANKS, Y_BANK2 = ps[:, 0:2, :], 2, 4, 6

        def bank(b, g):
            return ps[:, 4 * g + b, :].rearrange("p (k n) -> p k n", k=2)

        def y_bank(c, m):
            return ps[0:m, Y_BANK2 + c // 2, (c % 2) * D:(c % 2) * D + D]

        S = {n: sem(n) for n in """
            adj_loaded x_loaded consts_in eb1_loaded consts_made
            adj_t_ps y_ps h1_ps s2_ps h2_ps s3_ps o3_ps
            gw1_hi gw1_lo adj_hi adj_lo y_lo s2_lo s3_lo adj_t_sb y_sb h1_sb s2_sb h2_sb s3_sb x1_made
            xn_made xb3_made scale_made rough_made aggregates_made stats_made var_made newton_step cnt_made prefix_ps prefix_read run_made
            slots_made rows_made x1_stored spare_zeroed rows_known y_bias total_ps count_made widths_step widths_made b1_ps b1_sb dve_step pool_step
            xt_ps xt_sb hid_ps gelu_done hid_hi hid_lo down_done xt_hi w1_hi w1_lo w2_hi y_made passed""".split()}
        rows_copied = [sem(f"rows_copied{k}") for k in range(K)]
        rows_sent = [sem(f"rows_sent{k}") for k in range(K)]
        y_sent = [sem(f"y_sent{u}") for u in range(U)]
        filled = [sem(f"filled{u}") for u in range(U)]
        xr_loaded = [sem(f"xr_loaded{u}") for u in range(U)]
        w1_loaded = [sem(f"w1_loaded{u}") for u in range(U)]
        w2_loaded = [sem(f"w2_loaded{h}") for h in range(2)]
        w2_lo = [sem(f"w2_lo{h}") for h in range(2)]
        b2_loaded = [sem(f"b2_loaded{s}") for s in range(2)]
        N_CONSTS = 8

        block = ctx.enter_context(nc.Block())

        def expert(j, u):
            return 2 * j + u // 2 + HALF * (u % 2)

        def later(j, u, d):
            return j + (u + d) // U, (u + d) % U

        def uses(j, u):
            return 2 * j + u // 2 + 1

        def rounds_sent(eng, j, u, d):
            at, place = later(j, u, d)
            eng.wait_ge(y_sent[place], SENT * (at + 1))

        def counts_of(eng, which, j, ahead):
            n = U + (0 if is_last(j, E // U) else ahead)
            return nc.values_load_multi_w_load_instructions(
                count[0:1, bass.ds(U * j, n)], engines=(which,), min_val=0, max_val=CAP)[1]

        def by_width(eng, n, body):
            with eng.If(n < WIDTHS[0] + 1):
                body(WIDTHS[0])
            with eng.Else():
                with eng.If(n < WIDTHS[2] + 1):
                    with eng.If(n < WIDTHS[1] + 1):
                        body(WIDTHS[1])
                    with eng.Else():
                        body(WIDTHS[2])
                with eng.Else():
                    body(WIDTHS[3])

        def rounds(eng, body):
            body(0)
            with eng.Fori(1, E // U - 1) as j:
                body(j)
            body(E // U - 1)

        def pairs(eng, body):
            body(0)
            with eng.Fori(1, PAIRS - 1) as i:
                body(i)
            body(PAIRS - 1)

        def passed(eng):
            eng.sem_inc(S["passed"], 1)

        def is_first(i):
            return isinstance(i, int) and i == 0

        def is_last(i, n):
            return isinstance(i, int) and i == n - 1

        @block.sync
        def _(sp):
            def load_x(i):
                sp.dma_start(x_in[:, :, :], x_tok[bass.ds(i * 2 * N, 2 * N), :].rearrange(
                    "(t p) d -> p t d", p=P)).then_inc(S["x_loaded"], 16)

            def load_adj(i):
                sp.dma_start(adj_in[:, :, :], adj_tok[bass.ds(i * 2 * N, 2 * N), :].rearrange(
                    "(t p) d -> p t d", p=P)).then_inc(S["adj_loaded"], 16)

            def store_x1(i):
                sp.wait_ge(S["x1_made"], 2 * i + 2)
                sp.dma_start(out[bass.ds(i * 2 * N, 2 * N), :].rearrange("(t p) d -> p t d", p=P),
                             x1[:, :, :]).then_inc(S["x1_stored"], 16)

            def load_w1(j, u):
                sp.dma_start(w1_sb[:, u, :, :], ew1[expert(j, u)].rearrange(
                    "(k p) f -> p k f", p=P)).then_inc(w1_loaded[u], 16)

            def load_w2(j, u, h):
                sp.dma_start(w2_half[:, h, :, :], ew2[expert(j, u), h * F // 2:(h + 1) * F // 2, :].rearrange(
                    "(f p) d -> p f d", p=P)).then_inc(w2_loaded[h], 16)

            def load_b2(j, u):
                sp.dma_start(eb2_bc[:, u % 2, :], eb2[expert(j, u), :].partition_broadcast(
                    P)).then_inc(b2_loaded[u % 2], 16)

            load_x(0)
            load_adj(0)
            sp.dma_start(gw1_sb[:, :, :], gw1.rearrange("(k p) d -> p k d", p=P)).then_inc(S["consts_in"], 16)
            with nc.allow_non_contiguous_dma(reason="256 bias values, once"):
                sp.dma_start(gb1_sb[:, :], gb1.rearrange("(k p) -> p k", p=P)).then_inc(S["consts_in"], 16)
                sp.dma_start(gb2_sb[:, :], gb2.rearrange("(k p) -> p k", p=P)).then_inc(S["consts_in"], 16)
            sp.dma_start(gw2_sb[:, :, :], gw2.rearrange("(k p) d -> p k d", p=P)).then_inc(S["consts_in"], 16)
            sp.dma_start(gw3_sb[:, :, :], gw3.rearrange("(k p) d -> p k d", p=P)).then_inc(S["consts_in"], 16)
            sp.dma_start(gb3_bc[:, :], gb3.partition_broadcast(P)).then_inc(S["consts_in"], 16)
            for k in range(K):
                sp.dma_start(hash_bc[:, k, :], w_hash[k, :].partition_broadcast(P)).then_inc(S["consts_in"], 16)
            sp.dma_start(eb1_in, eb1).then_inc(S["eb1_loaded"], 16)
            sp.wait_ge(S["consts_made"], 1)
            sp.dma_start(out[T:T + SPARE, :].rearrange("(c p) d -> p c d", p=P),
                         xr[:, 0, :, 0:D]).then_inc(S["spare_zeroed"], 16)
            for h in range(2):
                load_w2(0, 0, h)
            for u in range(3):
                load_w1(0, u)
            load_b2(0, 0)
            with sp.Fori(1, PAIRS) as i:
                sp.wait_ge(S["adj_t_ps"], 2 * i)
                load_adj(i)
                sp.wait_ge(S["xn_made"], 2 * i)
                sp.wait_ge(S["xb3_made"], i)
                load_x(i)
                store_x1(i - 1)
            store_x1(PAIRS - 1)

            def fill(j, u, n):
                sp.dma_start(rows_hbm[bass.ds(expert(j, u) * STRIDE + n, FILL), :],
                             empty_row[:, :]).then_inc(filled[u], 16)

            def load_rows(j, u, n):
                row = expert(j, u) * STRIDE
                sp.wait_ge(filled[u], 16 * (j + 1))
                passed(sp)

                def body(w):
                    full, rest = w // P, w % P
                    if full:
                        sp.dma_start(xr[:, u, 0:full, :], rows_hbm[bass.ds(row, full * P), :].rearrange(
                            "(c p) d -> p c d", p=P)).then_inc(xr_loaded[u], 16 if rest else 32)
                    if rest:
                        sp.dma_start(xr[0:rest, u, full, :], rows_hbm[bass.ds(
                            row + full * P, rest), :]).then_inc(xr_loaded[u], 16 if full else 32)
                by_width(sp, n, body)

            sp.wait_ge(S["count_made"], 1)
            passed(sp)
            first_counts = counts_of(sp, mybir.EngineType.SP, 0, U)
            for u in range(U):
                fill(0, u, first_counts[u])
            sp.wait_ge(S["spare_zeroed"], 16)
            for k in range(K):
                sp.wait_ge(rows_sent[k], 16 * NT)
            passed(sp)
            for u in range(3):
                load_rows(0, u, first_counts[u])

            def round_of_loads(j):
                n = first_counts if is_first(j) else counts_of(sp, mybir.EngineType.SP, j, U)
                for u in range(U):
                    i = U * j + u
                    if not (is_last(j, E // U) and u == 3):
                        for h in range(2):
                            sp.wait_ge(w2_lo[h], i + 1)
                            load_w2(*later(j, u, 1), h)
                        if not (is_first(j) and u == 0):
                            sp.wait_ge(S["y_bias"], i)
                        load_b2(*later(j, u, 1))
                    if not is_last(j, E // U):
                        fill(*later(j, u, U), n[u + U])
                    if not (is_last(j, E // U) and u >= 1):
                        if not (is_first(j) and u == 0):
                            sp.wait_ge(S["hid_ps"], JF * i)
                        load_w1(*later(j, u, 3))
                        if not (is_first(j) and u == 0):
                            sp.wait_ge(S["y_made"], i)
                            passed(sp)
                        load_rows(*later(j, u, 3), n[u + 3])
            rounds(sp, round_of_loads)

            for u in range(U):
                sp.wait_ge(y_sent[u], SENT * (E // U))

        @block.gpsimd
        def _(pool):
            nc.gpsimd.memset(xr[:, :, :, :], 0.0)
            nc.gpsimd.memset(ones_f[:, :], 1.0)
            nc.gpsimd.memset(ones_b[:, :], 1.0)
            nc.gpsimd.memset(run_cnt[:, :], 0.0)
            nc.gpsimd.memset(minus_half[:, :], -0.5)
            nc.gpsimd.memset(payload[:, :, :, :], 1.0 / K)
            nc.gpsimd.memset(empty_row[:, :], 0.0).then_inc(S["pool_step"], 1)
            pool.wait_ge(S["pool_step"], 1)
            nc.gpsimd.memset(empty_row[:, ID:ID + 1], float(T))
            nc.gpsimd.affine_select(out=ident[:, :], in_=ones_f[:, :], compare_op=ALU.is_equal, fill=0.0, base=0,
                                    pattern=[[-1, P]], channel_multiplier=1)
            nc.gpsimd.affine_select(out=before[:, :], in_=ones_b[:, :], compare_op=ALU.is_gt, fill=0.0, base=0,
                                    pattern=[[1, P]], channel_multiplier=-1)
            nc.gpsimd.iota(expert_no[:, :], pattern=[[1, E]], base=0, channel_multiplier=0,
                           allow_small_or_imprecise_dtypes=True)
            nc.gpsimd.iota(spare_no[:, :], pattern=[[P, CB]], base=0, channel_multiplier=1,
                           allow_small_or_imprecise_dtypes=True)
            nc.gpsimd.iota(token_no[:, :, :], pattern=[[TPP * P, PAIRS], [P, TPP]], base=0, channel_multiplier=1,
                           allow_small_or_imprecise_dtypes=True).then_inc(S["consts_made"], 1)

            def add_b3(i):
                pool.wait_ge(S["x_loaded"], 16 * (i + 1))
                if not is_first(i):
                    pool.wait_ge(S["x1_made"], 2 * i)
                nc.gpsimd.tensor_tensor(xb3[:, :, :], x_in[:, :, :],
                                        gb3_bc[:, :].unsqueeze(1).to_broadcast([P, TPP, D]),
                                        ALU.add).then_inc(S["xb3_made"], 1)

            def count_pair(i):
                pool.wait_ge(S["prefix_ps"], i + 1)
                nc.gpsimd.tensor_tensor(two_cnt[:, :, :], tile_cnt[:, 0:2, :], tile_cnt[:, 2:4, :],
                                        ALU.add).then_inc(S["pool_step"], 1)
                pool.wait_ge(S["pool_step"], 2 * i + 2)
                nc.gpsimd.tensor_tensor(run_cnt[:, :], run_cnt[:, :], two_cnt[:, 0, :], ALU.add).then_inc(S["pool_step"], 1)
                pool.wait_ge(S["pool_step"], 2 * i + 3)
                nc.gpsimd.tensor_tensor(run_cnt[:, :], run_cnt[:, :], two_cnt[:, 1, :], ALU.add).then_inc(S["run_made"], 1)
                pool.wait_ge(S["run_made"], i + 1)

            def send_rows(i, k, tiles=range(TPP)):
                pool.wait_ge(rows_copied[k], i + 1)
                pool.wait_ge(S["slots_made"], i + 1)
                passed(pool)
                for t in tiles:
                    c = k * TPP + t
                    nc.gpsimd.indirect_dma_start(
                        out=rows_hbm, out_offset=bass.IndirectOffsetOnAxis(ap=slot[:, c:c + 1], axis=0),
                        in_=payload[:, k, t, :], in_offset=None, bounds_check=E * STRIDE - 1,
                        oob_is_err=False).then_inc(rows_sent[k], 16)

            def rough_rstd(which, n):
                pool.wait_ge(S["var_made"], n)
                return nc.gpsimd.tensor_tensor(rstd[:, which, 0, :], var_e[:, which, :], minus_half[:, :], ALU.pow)

            def first_scales(i, n):
                r = rstd[:, 0, :, :]

                def step(ins, k):
                    ins.then_inc(S["newton_step"], 1)
                    pool.wait_ge(S["newton_step"], 6 * i + k)

                step(rough_rstd(0, n), 1)
                step(nc.gpsimd.tensor_tensor(r[:, 1, :], r[:, 0, :], r[:, 0, :], ALU.mult), 2)
                step(nc.gpsimd.tensor_tensor(r[:, 2, :], r[:, 1, :], var_e[:, 0, :], ALU.mult), 3)
                passed(pool)
                step(nc.gpsimd.tensor_scalar(r[:, 1, :], r[:, 2, :], -0.5, 1.5, ALU.mult, ALU.add), 4)
                step(nc.gpsimd.tensor_tensor(r[:, 3, :], r[:, 0, :], r[:, 1, :], ALU.mult), 5)
                step(nc.gpsimd.tensor_tensor(shift[:, :], mv[:, 0, :, 0], r[:, 3, :], ALU.mult), 6)
                passed(pool)
                nc.gpsimd.tensor_scalar(shift[:, :], shift[:, :], -1.0, None, ALU.mult).then_inc(S["scale_made"], 1)

            def second_scales(n):
                rough_rstd(1, n).then_inc(S["rough_made"], 1)

            first_scales(0, 1)
            pool.wait_ge(S["consts_in"], 16 * N_CONSTS)

            def adjacency_lo(i):
                for g in range(2):
                    pool.wait_ge(S["adj_hi"], 2 * i + g + 1)
                    nc.gpsimd.tensor_tensor(adj_lo[:, g, :, :], adj_t[:, g, :, :], adj_hi[:, g, :, :].bitcast(fp32),
                                            ALU.subtract).then_inc(S["adj_lo"], 1)

            def pair_of_graphs(i):
                if not is_first(i):
                    second_scales(2 * i + 1)
                    if not (isinstance(i, int) and i == 1):
                        send_rows(i - 2, 0, range(TPP - 1, TPP))
                add_b3(i)
                adjacency_lo(i)
                if not is_first(i) and not (isinstance(i, int) and i == 1):
                    send_rows(i - 2, 1)
                if not is_last(i, PAIRS):
                    first_scales(i + 1, 2 * i + 2)
                if not is_first(i):
                    count_pair(i - 1)
                    send_rows(i - 1, 0, range(TPP - 1))
            for i in range(2):
                pair_of_graphs(i)
            with pool.Fori(2, PAIRS - 1) as i:
                pair_of_graphs(i)
            pair_of_graphs(PAIRS - 1)
            second_scales(2 * PAIRS)
            send_rows(PAIRS - 2, 0, range(TPP - 1, TPP))
            send_rows(PAIRS - 2, 1)

            def w1_lo_parts(j, u):
                for q in range(4):
                    pool.wait_ge(S["w1_hi"], 2 * (U * j + u) + q // 2 + 1)
                    cols = slice(q * F // 4, (q + 1) * F // 4)
                    nc.gpsimd.tensor_tensor(w1_lo[:, u % 2, :, cols], w1_sb[:, u, :, cols],
                                            w1_hi[:, u % 2, :, cols].bitcast(fp32), ALU.subtract).then_inc(S["w1_lo"], 1)

            def w2_lo_half(j, u):
                pool.wait_ge(S["w2_hi"], 2 * (U * j + u) + 2)
                nc.gpsimd.tensor_tensor(w2_low[:, u % 2, JF // 2:, :], w2_half[:, 1, :, :],
                                        w2_hi[:, u % 2, JF // 2:, :].bitcast(fp32), ALU.subtract).then_inc(w2_lo[1], 1)

            w1_lo_parts(0, 0)
            count_pair(PAIRS - 1)
            for k in range(K):
                send_rows(PAIRS - 1, k)
            w2_lo_half(0, 0)

            pool.wait_ge(S["x1_stored"], 16 * PAIRS)
            pool.wait_ge(S["spare_zeroed"], 16)
            pool.wait_ge(S["count_made"], 1)
            passed(pool)

            def send_results(j, u, n):
                def body(w):
                    if not (is_first(j) and u == 0):
                        rounds_sent(pool, j, u, -1)
                    pool.wait_ge(S["y_made"], U * j + u + 1)
                    passed(pool)
                    cs = blocks(w)
                    for c, m in cs:
                        nc.gpsimd.indirect_dma_start(
                            out=out, out_offset=bass.IndirectOffsetOnAxis(ap=row_i[0:m, u, c:c + 1], axis=0),
                            in_=y_out[0:m, u % 2, c, :], in_offset=None, bounds_check=T + SPARE - 1,
                            compute_op=ALU.add).then_inc(y_sent[u], SENT - 16 * (len(cs) - 1) if c == 0 else 16)
                by_width(pool, n, body)

            def w1_lo_where_split(j, u, n):
                with pool.If(n > PLAIN):
                    w1_lo_parts(j, u)
                with pool.Else():
                    pool.wait_ge(S["w1_hi"], 2 * (U * j + u) + 2)
                    passed(pool)
                    for q in range(4):
                        pool.drain().then_inc(S["w1_lo"], 1)

            first_counts = counts_of(pool, mybir.EngineType.Pool, 0, 2)
            w1_lo_where_split(0, 1, first_counts[1])

            def round_of_sends(j):
                n = first_counts if is_first(j) else counts_of(pool, mybir.EngineType.Pool, j, 2)
                for u in range(U):
                    if not (is_last(j, E // U) and u == 3):
                        w2_lo_half(*later(j, u, 1))
                    if not (is_last(j, E // U) and u >= 2):
                        w1_lo_where_split(*later(j, u, 2), n[u + 2])
                    send_results(j, u, n[u])
            rounds(pool, round_of_sends)

        @block.scalar
        def _(act):
            def out_of_psum(to, frm, ready, done, g_no):
                act.wait_ge(ready, g_no + 1)
                nc.scalar.copy(to, frm).then_inc(done, 1)

            def relu_out(to, g, b, bias, ready, done, g_no):
                act.wait_ge(ready, g_no + 1)
                for hb in range(KD):
                    last = nc.scalar.activation(to[:, g, hb, :], bank(b, g)[:, hb, :], ACT.Relu,
                                                bias=bias[:, hb:hb + 1])
                last.then_inc(done, 1)

            def normalise(i, ts):
                if ts[0] == 0:
                    act.wait_ge(S["scale_made"], i + 1)
                for t in ts:
                    last = nc.scalar.activation(xn[:, t, :], x_in[:, t, :], ACT.Identity,
                                                scale=rstd[:, 0, 3, t:t + 1], bias=shift[:, t:t + 1])
                last.then_inc(S["xn_made"], 1)

            normalise(0, (0, 1))
            normalise(0, (2, 3))

            def copy_rows(i, k):
                if k == 0:
                    act.wait_ge(S["rows_made"], i + 1)
                    if not is_first(i):
                        act.wait_ge(rows_copied[1], i)
                else:
                    act.wait_ge(rows_copied[0], i + 1)
                if not is_first(i):
                    act.wait_ge(rows_sent[k], 16 * TPP * i)
                nc.scalar.copy(payload[:, k, :, 0:D], rows[:, :, :] if k == 0 else payload[:, 0, :, 0:D]).then_inc(
                    rows_copied[k], 1)

            def adjacencies_out(i):
                for g in range(2):
                    out_of_psum(adj_t[:, g, :, :], bank(T_BANK, g), S["adj_t_ps"], S["adj_t_sb"], 2 * i + g)

            adjacencies_out(0)
            act.wait_ge(S["consts_in"], 16 * N_CONSTS)
            nc.scalar.copy(gw1_hi[:, :, :], gw1_sb[:, :, :]).then_inc(S["gw1_hi"], 1)
            act.wait_ge(S["b1_ps"], 1)
            nc.scalar.copy(eb1_t[:, :, :].rearrange("p f e -> p (f e)"), ps[:, 3, :]).then_inc(S["b1_sb"], 1)

            def pair_of_graphs(i):
                for g in range(2):
                    out_of_psum(y_hi[:, g, :, :], bank(Y_BANK, g), S["y_ps"], S["y_sb"], 2 * i + g)
                for g in range(2):
                    if not is_first(i):
                        act.wait_ge(S["o3_ps"], 2 * (i - 1) + g + 1)
                    out_of_psum(adj_hi[:, g, :, :], bank(T_BANK, g), S["adj_t_ps"], S["adj_hi"], 2 * i + g)
                for g in range(2):
                    relu_out(h1_t, g, H1_BANK, gb1_sb, S["h1_ps"], S["h1_sb"], 2 * i + g)
                for g in range(2):
                    out_of_psum(s2_hi[:, g, :, :], bank(S2_BANK, g), S["s2_ps"], S["s2_sb"], 2 * i + g)
                    if g == 0 and not is_first(i) and not (isinstance(i, int) and i == 1):
                        copy_rows(i - 2, 1)
                for g in range(2):
                    relu_out(h2_t, g, H2_BANK, gb2_sb, S["h2_ps"], S["h2_sb"], 2 * i + g)
                for g in range(2):
                    out_of_psum(s3_hi[:, g, :, :], bank(S3_BANK, g), S["s3_ps"], S["s3_sb"], 2 * i + g)
                if not is_first(i):
                    copy_rows(i - 1, 0)
                if not is_last(i, PAIRS):
                    for g in range(2):
                        normalise(i + 1, (2 * g, 2 * g + 1))
                    adjacencies_out(i + 1)
            for i in range(2):
                pair_of_graphs(i)
            with act.Fori(2, PAIRS - 1) as i:
                pair_of_graphs(i)
            pair_of_graphs(PAIRS - 1)
            copy_rows(PAIRS - 2, 1)

            def w2_hi_parts(j, u):
                i = U * j + u
                if not (is_first(j) and u < 2):
                    act.wait_ge(S["down_done"], i - 1)
                for h in range(2):
                    act.wait_ge(w2_loaded[h], 16 * (i + 1))
                    nc.scalar.copy(w2_hi[:, u % 2, h * JF // 2:(h + 1) * JF // 2, :],
                                   w2_half[:, h, :, :]).then_inc(S["w2_hi"], 1)

            act.wait_ge(w1_loaded[0], 16)
            for h in range(2):
                cols = slice(h * F // 2, (h + 1) * F // 2)
                nc.scalar.copy(w1_hi[:, 0, :, cols], w1_sb[:, 0, :, cols]).then_inc(S["w1_hi"], 1)
            w2_hi_parts(0, 0)
            for k in range(K):
                copy_rows(PAIRS - 1, k)

            act.wait_ge(S["count_made"], 1)
            act.wait_ge(S["b1_sb"], 1)
            passed(act)

            def round_of_gelus(j):
                n = counts_of(act, mybir.EngineType.Activation, j, 0)
                for u in range(U):
                    i = U * j + u
                    bias = bass.ds(expert(j, u), 1)

                    def body(w):
                        for f in range(JF):
                            if f == 0 and w > PLAIN and not (is_first(j) and u == 0):
                                act.wait_ge(S["down_done"], i)
                            act.wait_ge(S["hid_ps"], JF * i + f + 1)
                            if not (is_first(j) and u == 0 and f < HIDDEN_RING):
                                act.wait_ge(S["hid_lo"], JF // 2 * i + (f - HIDDEN_RING) // 2 + 1)
                            h_ps = ps[:, H_BANK + f % H_BANKS, 0:w]
                            last = nc.scalar.activation(hid[:, f % HIDDEN_RING, 0:w], h_ps, ACT.Gelu,
                                                        bias=eb1_t[:, f, bias])
                            if w > PLAIN:
                                last = nc.scalar.activation(h_hi[:, f, 0:w], h_ps, ACT.Gelu, bias=eb1_t[:, f, bias])
                            last.then_inc(S["gelu_done"], 1)
                        act.wait_ge(b2_loaded[u % 2], 16 * uses(j, u))
                        if not (is_first(j) and u == 0):
                            act.wait_ge(S["y_made"], i)
                        for c, m in blocks(P if w <= P else CAP):
                            last = nc.scalar.activation(y_bias[0:m, c, :], eb2_bc[0:m, u % 2, :], ACT.Copy,
                                                        scale=xr[0:m, u, c, WEIGHT:WEIGHT + 1])
                        last.then_inc(S["y_bias"], 1)
                    by_width(act, n[u], body)
                    if not (is_last(j, E // U) and u == 3):
                        w2_hi_parts(*later(j, u, 1))
            rounds(act, round_of_gelus)

        @block.vector
        def _(dve):
            PER_PAIR = 4 + 14
            made = {"base": 0, "n": 0}

            def step(ins, between=lambda: None):
                made["n"] += 1
                ins.then_inc(S["dve_step"], 1)
                between()
                dve.wait_ge(S["dve_step"], made["base"] + made["n"])

            def tile_stats(t, src):
                ins = nc.vector.bn_stats(stats[:, t, :], src(t))
                if t == TPP - 1:
                    ins.then_inc(S["stats_made"], 1)

            def aggregates(which, n):
                dve.wait_ge(S["stats_made"], n)
                passed(dve)
                for t in range(TPP):
                    last = nc.vector.bn_aggr(mv[:, which, t, :], stats[:, t, :])
                last.then_inc(S["aggregates_made"], 1)

            def add_eps(which, n):
                dve.wait_ge(S["aggregates_made"], n)
                nc.vector.tensor_scalar(var_e[:, which, :], mv[:, which, :, 1], EPS, None,
                                        ALU.add).then_inc(S["var_made"], 1)

            def variances(which, src, n, between=lambda: None):
                for t in range(TPP):
                    if t == TPP // 2:
                        between()
                    tile_stats(t, src)
                aggregates(which, n)
                add_eps(which, n)

            def x_tile(t):
                return x_in[:, t, :]

            def lo_part(lo, frm, hi, hi_made, made_now, i, g):
                dve.wait_ge(S[hi_made], 2 * i + g + 1)
                nc.vector.tensor_tensor(lo[:, g, :, :], frm, hi[:, g, :, :].bitcast(fp32),
                                        ALU.subtract).then_inc(S[made_now], 1)

            def y_lo_of(i, g):
                lo_part(y_lo, bank(Y_BANK, g), y_hi, "y_sb", "y_lo", i, g)

            def s2_lo_of(i, g):
                lo_part(s2_lo, bank(S2_BANK, g), s2_hi, "s2_sb", "s2_lo", i, g)

            def s3_lo_of(i, g):
                lo_part(s3_lo, bank(S3_BANK, g), s3_hi, "s3_sb", "s3_lo", i, g)

            def await_x(i):
                dve.wait_ge(S["x_loaded"], 16 * (i + 1))
                if not is_first(i):
                    dve.wait_ge(S["xn_made"], 2 * i)

            def residual(i):
                dve.wait_ge(S["xb3_made"], i + 1)
                if not is_first(i):
                    dve.wait_ge(S["x1_stored"], 16 * i)
                for g in range(2):
                    dve.wait_ge(S["o3_ps"], 2 * i + g + 1)
                    nc.vector.tensor_tensor(x1[:, 2 * g:2 * g + 2, :], bank(O3_BANK, g),
                                            xb3[:, 2 * g:2 * g + 2, :], ALU.add).then_inc(S["x1_made"], 1)
                dve.wait_ge(S["x1_made"], 2 * i + 2)
                passed(dve)

            def second_norm(i):
                if is_last(i, PAIRS):
                    variances(1, lambda t: x1[:, t, :], 2 * PAIRS)
                else:
                    variances(1, lambda t: x1[:, t, :], 2 * i + 3, lambda: y_lo_of(i + 1, 0))
                    y_lo_of(i + 1, 1)
                dve.wait_ge(S["rough_made"], i + 1)
                r = rstd[:, 1, :, :]
                step(nc.vector.tensor_tensor(r[:, 1, :], r[:, 0, :], r[:, 0, :], ALU.mult))
                step(nc.vector.tensor_tensor(r[:, 2, :], r[:, 1, :], var_e[:, 1, :], ALU.mult))
                step(nc.vector.tensor_scalar(r[:, 1, :], r[:, 2, :], -0.5, 1.5, ALU.mult, ALU.add))
                step(nc.vector.tensor_tensor(r[:, 3, :], r[:, 0, :], r[:, 1, :], ALU.mult))
                if not is_first(i):
                    dve.wait_ge(rows_copied[0], i)
                for t in range(TPP):
                    last = nc.vector.tensor_scalar(rows[:, t, :], x1[:, t, :], mv[:, 1, t, 0:1],
                                                   rstd[:, 1, 3, t:t + 1], ALU.subtract, ALU.mult)
                last.then_inc(S["rows_made"], 1)
                dve.wait_ge(S["rows_made"], i + 1)
                def scores(cs):
                    for c in cs:
                        ins = nc.vector.tensor_tensor_reduce(
                            out=prod[:, c, :], in0=rows[:, c % TPP, :], in1=hash_bc[:, c // TPP, :],
                            scale=1.0, scalar=0.0, op0=ALU.mult, op1=ALU.add, accum_out=score[:, c:c + 1])
                    return ins

                if is_last(i, PAIRS):
                    last = scores(range(K * TPP))
                else:
                    scores(range(3))
                    s2_lo_of(i + 1, 0)
                    scores(range(3, 6))
                    s2_lo_of(i + 1, 1)
                    last = scores(range(6, K * TPP))
                step(last)
                fillers = [lambda: None] * 6
                if not is_last(i, PAIRS) and not is_last(i, PAIRS - 1):
                    await_x(i + 2)
                    n = 2 * i + 4
                    fillers = [lambda t=t: tile_stats(t, x_tile) for t in range(TPP)]
                    fillers += [lambda: aggregates(0, n), lambda: add_eps(0, n)]
                step(nc.vector.tensor_scalar(floor_i[:, 0, :], score[:, :], BUCKET_SCALE, None, ALU.mult), fillers[0])
                step(nc.vector.tensor_copy(floor_f[:, 0, :], floor_i[:, 0, :]), fillers[1])
                step(nc.vector.scalar_tensor_tensor(out=floor_f[:, 1, :], in0=score[:, :], scalar=BUCKET_SCALE,
                                                    in1=floor_f[:, 0, :], op0=ALU.mult, op1=ALU.is_lt), fillers[2])
                step(nc.vector.tensor_tensor(floor_f[:, 2, :], floor_f[:, 0, :], floor_f[:, 1, :], ALU.subtract),
                     fillers[3])
                step(nc.vector.tensor_copy(floor_i[:, 1, :], floor_f[:, 2, :]), fillers[4])
                step(nc.vector.tensor_scalar(floor_i[:, 2, :], floor_i[:, 1, :], E - 1, None, ALU.bitwise_and),
                     fillers[5])
                step(nc.vector.tensor_copy(bucket[:, :], floor_i[:, 2, :]))
                step(nc.vector.tensor_tensor(same[:, :], bucket[:, 0:TPP], bucket[:, TPP:2 * TPP], ALU.is_equal))
                step(nc.vector.tensor_tensor(
                    onehot[:, :, :, :].rearrange("p k t e -> p (k t) e"),
                    bucket[:, :].unsqueeze(2).to_broadcast([P, K * TPP, E]),
                    expert_no[:, :].unsqueeze(1).to_broadcast([P, K * TPP, E]), ALU.is_equal))
                if not is_first(i):
                    dve.wait_ge(S["run_made"], i)
                nc.vector.tensor_tensor(tile_cnt[:, :, :], onehot[:, 0, :, :], onehot[:, 1, :, :],
                                        ALU.add).then_inc(S["cnt_made"], 1)

            def slots(i):
                dve.wait_ge(S["prefix_ps"], i + 1)
                if not is_first(i):
                    for k in range(K):
                        dve.wait_ge(rows_sent[k], 16 * TPP * i)
                nc.vector.tensor_tensor(
                    picked[:, :].rearrange("p (k c) -> p k c", k=K),
                    onehot[:, :, :, :].rearrange("p k t e -> p k (t e)"),
                    PREFIX.unsqueeze(1).to_broadcast([P, K, TPP * E]), ALU.mult).then_inc(S["prefix_read"], 1)
                dve.wait_ge(S["prefix_read"], i + 2)
                step(nc.vector.tensor_reduce(pos[:, 0, :], picked[:, :].rearrange("p (c e) -> p c e", e=E), AX.X, ALU.add))
                step(nc.vector.tensor_tensor(pos[:, 0, TPP:2 * TPP], pos[:, 0, TPP:2 * TPP], same[:, :], ALU.add))
                nc.vector.scalar_tensor_tensor(out=pos[:, 1, :], in0=bucket[:, :], scalar=float(STRIDE),
                                               in1=pos[:, 0, :], op0=ALU.mult, op1=ALU.add)
                nc.vector.tensor_scalar(pos[:, 2, :], pos[:, 0, :], float(CAP), DROPPED, ALU.is_ge, ALU.mult)
                step(nc.vector.scalar_tensor_tensor(out=both[:, 0, :], in0=pos[:, 0, TPP:2 * TPP], scalar=float(CAP),
                                                    in1=same[:, :], op0=ALU.is_lt, op1=ALU.mult))
                nc.vector.tensor_scalar(both[:, 1, :], same[:, :], float(T), None, ALU.mult)
                number = token_no[:, bass.ds(i, 1), :].rearrange("p o t -> p (o t)")
                nc.vector.tensor_scalar(payload[:, 0, :, WEIGHT], both[:, 0, :], 1.0 / K, 1.0 / K, ALU.mult, ALU.add)
                nc.vector.tensor_copy(payload[:, 0, :, ID], number)
                step(nc.vector.tensor_tensor(slot[:, :], pos[:, 1, :], pos[:, 2, :], ALU.add))
                nc.vector.tensor_tensor(payload[:, 1, :, ID], both[:, 1, :], number,
                                        ALU.max).then_inc(S["slots_made"], 1)
                dve.wait_ge(S["slots_made"], i + 1)

            dve.sem_inc(S["prefix_read"], 1)
            await_x(0)
            variances(0, x_tile, 1)
            dve.wait_ge(S["gw1_hi"], 1)
            nc.vector.tensor_tensor(gw1_lo[:, :, :], gw1_sb[:, :, :], gw1_hi[:, :, :].bitcast(fp32),
                                    ALU.subtract).then_inc(S["gw1_lo"], 1)
            for g in range(2):
                y_lo_of(0, g)

            def pair_of_graphs(i):
                at = made["n"]
                if not isinstance(i, int):
                    made["base"] = (i - 1) * PER_PAIR
                if not is_first(i):
                    for g in range(2):
                        s3_lo_of(i, g)
                    slots(i - 1)
                else:
                    for g in range(2):
                        s2_lo_of(i, g)
                    await_x(1)
                    variances(0, x_tile, 2)
                    for g in range(2):
                        s3_lo_of(i, g)
                residual(i)
                second_norm(i)
                if not isinstance(i, int):
                    assert made["n"] - at == PER_PAIR, (made["n"] - at, PER_PAIR)
                    made["base"], made["n"] = 0, made["n"] + (PAIRS - 4) * PER_PAIR
            pair_of_graphs(0)
            with dve.Fori(1, PAIRS - 2) as i:
                pair_of_graphs(i)
            pair_of_graphs(PAIRS - 2)
            pair_of_graphs(PAIRS - 1)
            slots(PAIRS - 1)

            dve.wait_ge(S["total_ps"], 1)
            nc.vector.tensor_scalar(count[:, :].rearrange("p (a h) -> p h a", h=2),
                                    COUNTS.rearrange("p (h a) -> p h a", h=2), float(CAP), None,
                                    ALU.min).then_inc(S["count_made"], 1)
            dve.wait_ge(S["count_made"], 1)

            def width_step(ins, n):
                ins.then_inc(S["widths_step"], 1)
                dve.wait_ge(S["widths_step"], n)

            width_step(nc.vector.tensor_scalar(width_no[:, 0, :], count[:, :], float(WIDTHS[0]), None, ALU.is_gt), 1)
            for at in (1, 2):
                width_step(nc.vector.scalar_tensor_tensor(
                    out=width_no[:, at, :], in0=count[:, :], scalar=float(WIDTHS[at]), in1=width_no[:, at - 1, :],
                    op0=ALU.is_gt, op1=ALU.add), at + 1)
            of_place = width_no[:, 2, :].rearrange("p (j u) -> p u j", u=U)
            for u in range(U - 2, -1, -1):
                frm = of_place[:, U - 1, :] if u == U - 2 else widths_of[:, (u + 1) % 2, :]
                to = round_widths[:, :] if u == 0 else widths_of[:, u % 2, :]
                width_step(nc.vector.scalar_tensor_tensor(out=to, in0=frm, scalar=4.0, in1=of_place[:, u, :],
                                                          op0=ALU.mult, op1=ALU.add), U + 2 - u)
            dve.sem_inc(S["widths_made"], 1)

            def hidden_parts(j, u, n):
                i = U * j + u

                def body(w):
                    for g in range(JF // 2):
                        fs = slice(2 * g, 2 * g + 2)
                        ring = hid[:, 2 * g % HIDDEN_RING:2 * g % HIDDEN_RING + 2, 0:w]
                        if g == 0 and w <= PLAIN and not (is_first(j) and u == 0):
                            dve.wait_ge(S["down_done"], i)
                        dve.wait_ge(S["gelu_done"], JF * i + 2 * g + 2)
                        if w <= PLAIN:
                            nc.vector.tensor_copy(h_hi[:, fs, 0:w], ring).then_inc(S["hid_hi"], 1)
                        else:
                            dve.sem_inc(S["hid_hi"], 1)
                        dve.wait_ge(S["hid_hi"], JF // 2 * i + g + 1)
                        nc.vector.tensor_tensor(h_lo[:, fs, 0:w], ring, h_hi[:, fs, 0:w].bitcast(fp32),
                                                ALU.subtract).then_inc(S["hid_lo"], 1)
                by_width(dve, n, body)

            def rows_out(j, u, n):
                i = U * j + u

                def body(w):
                    if not (is_first(j) and u < 2):
                        dve.wait_ge(S["hid_ps"], JF * (i - 1))
                    dve.wait_ge(S["xt_ps"], i + 1)
                    if w > PLAIN:
                        nc.vector.tensor_copy(xt_hi[:, u % 2, :, 0:w], XT_BANKS[:, :, 0:w]).then_inc(S["xt_hi"], 1)
                        dve.wait_ge(S["xt_hi"], i + 1)
                        nc.vector.tensor_tensor(xt_lo[:, u % 2, :, 0:w], XT_BANKS[:, :, 0:w],
                                                xt_hi[:, u % 2, :, 0:w].bitcast(fp32),
                                                ALU.subtract).then_inc(S["xt_sb"], 1)
                    else:
                        for k, done in enumerate((S["xt_hi"], S["xt_sb"])):
                            nc.vector.tensor_copy(xt[:, u % 2, k, 0:w], XT_BANKS[:, k, 0:w]).then_inc(done, 1)
                by_width(dve, n, body)

            def w1_hi_parts(j, u, n):
                with dve.If(n > PLAIN):
                    dve.wait_ge(w1_loaded[u], 16 * (j + 1))
                    for h in range(2):
                        cols = slice(h * F // 2, (h + 1) * F // 2)
                        nc.vector.tensor_copy(w1_hi[:, u % 2, :, cols], w1_sb[:, u, :, cols]).then_inc(S["w1_hi"], 1)
                with dve.Else():
                    for h in range(2):
                        dve.drain().then_inc(S["w1_hi"], 1)

            def w2_lo_half(j, u):
                dve.wait_ge(S["w2_hi"], 2 * (U * j + u) + 1)
                nc.vector.tensor_tensor(w2_low[:, u % 2, 0:JF // 2, :], w2_half[:, 0, :, :],
                                        w2_hi[:, u % 2, 0:JF // 2, :].bitcast(fp32), ALU.subtract).then_inc(w2_lo[0], 1)

            def results_out(j, u, n):
                i = U * j + u
                ids = xr[:, u, :, ID:ID + 1].rearrange("p c o -> p (c o)")
                dve.wait_ge(S["xt_ps"], i + 1)
                nc.vector.scalar_tensor_tensor(out=row_no[:, u % 2, :], in0=ids, scalar=float(T),
                                               in1=spare_no[:, :], op0=ALU.is_ge, op1=ALU.mult).then_inc(S["rows_known"], 1)
                if not (is_first(j) and u < 2):
                    rounds_sent(dve, j, u, -2)
                dve.wait_ge(S["rows_known"], i + 1)
                nc.vector.tensor_tensor(row_i[:, u, :], row_no[:, u % 2, :], ids, ALU.add)

                def weigh(c, m):
                    return nc.vector.scalar_tensor_tensor(
                        out=y_out[0:m, u % 2, c, :], in0=y_bank(c, m), scalar=xr[0:m, u, c, WEIGHT:WEIGHT + 1],
                        in1=y_bias[0:m, c, :], op0=ALU.mult, op1=ALU.add)

                def body(rows):
                    dve.wait_ge(S["y_bias"], i + 1)
                    dve.wait_ge(S["down_done"], i + 1)
                    for c, m in blocks(rows):
                        last = weigh(c, m)
                    last.then_inc(S["y_made"], 1)

                with dve.If(n < P + 1):
                    body(P)
                with dve.Else():
                    body(CAP)

            def one_count(j, u):
                return nc.values_load_multi_w_load_instructions(
                    count[0:1, bass.ds(U * j + u, 1)], engines=(mybir.EngineType.DVE,), min_val=0, max_val=CAP)[1][0]

            w2_lo_half(0, 0)
            first_counts = [one_count(0, 0), one_count(0, 1)]
            rows_out(0, 0, first_counts[0])
            rows_out(0, 1, first_counts[1])
            w1_hi_parts(0, 1, first_counts[1])

            def round_of_results(j):
                n = list(first_counts) if is_first(j) else [one_count(j, 0), one_count(j, 1)]
                for u in range(U):
                    hidden_parts(j, u, n[u])
                    if not (is_last(j, E // U) and u >= 2):
                        n.append(one_count(j, u + 2))
                        rows_out(*later(j, u, 2), n[u + 2])
                        w1_hi_parts(*later(j, u, 2), n[u + 2])
                    if not (is_last(j, E // U) and u == 3):
                        w2_lo_half(*later(j, u, 1))
                    results_out(j, u, n[u])
            rounds(dve, round_of_results)

        @block.tensor
        def _(pe):
            pe.wait_ge(S["consts_made"], 1)

            def product(to, lhs, rhs, done):
                for b in range(KD):
                    for k in range(KD):
                        last = nc.tensor.matmul(to[:, b, :], lhs(k, b), rhs(k), start=(k == 0), stop=(k == KD - 1))
                last.then_inc(done, 1)

            def half(b):
                return slice(b * P, b * P + P)

            def split_product(to, lhs, rhs, done):
                for b in range(KD):
                    for k in range(KD):
                        for at, (l, m) in enumerate(((0, 0), (0, 1), (1, 0))):
                            last = nc.tensor.matmul(to[:, b, :], lhs(l, k, b), rhs(m, k), start=(k == 0 and at == 0),
                                                    stop=(k == KD - 1 and at == 2))
                last.then_inc(done, 1)


            def prefix(i):
                pe.wait_ge(S["cnt_made"], i + 1)
                if not is_first(i):
                    pe.wait_ge(S["run_made"], i)
                nc.tensor.matmul(PREFIX, before[:, :], tile_cnt[:, :, :].rearrange("p t e -> p (t e)"),
                                 start=True, stop=False)
                for t in range(TPP - 1):
                    nc.tensor.matmul(PREFIX[:, (t + 1) * E:], ones_b[:, :],
                                     tile_cnt[:, t, :].unsqueeze(1).to_broadcast([P, TPP - 1 - t, E]),
                                     start=False, stop=False)
                nc.tensor.matmul(PREFIX, ones_b[:, :], run_cnt[:, :].unsqueeze(1).to_broadcast([P, TPP, E]),
                                 start=False, stop=True).then_inc(S["prefix_ps"], 1)

            def adjacencies_in(i):
                pe.wait_ge(S["adj_loaded"], 16 * (i + 1))
                for g in range(2):
                    for mb in range(KD):
                        for nb in range(KD):
                            last = nc.tensor.transpose(bank(T_BANK, g)[:, mb, half(nb)],
                                                       adj_in[:, 2 * g + nb, half(mb)], ident[:, :])
                    last.then_inc(S["adj_t_ps"], 1)

            adjacencies_in(0)
            pe.wait_ge(S["consts_in"], 16 * N_CONSTS)
            pe.wait_ge(S["eb1_loaded"], 16)
            for f in range(JF):
                last = nc.tensor.transpose(ps[:, 3, f * E:f * E + E], eb1_in[:, f * P:f * P + P], ident[0:E, 0:E])
            last.then_inc(S["b1_ps"], 1)

            def pair_of_graphs(i):
                for g in range(2):
                    pe.wait_ge(S["xn_made"], 2 * i + g + 1)
                    pe.wait_ge(S["adj_t_sb"], 2 * i + g + 1)
                    product(bank(Y_BANK, g), lambda k, b: xn[:, 2 * g + k, half(b)],
                            lambda k: adj_t[:, g, k, :], S["y_ps"])
                for g in range(2):
                    if is_first(i) and g == 0:
                        pe.wait_ge(S["gw1_lo"], 1)
                    pe.wait_ge(S["y_lo"], 2 * i + g + 1)
                    if not is_first(i):
                        pe.wait_ge(S["x1_made"], 2 * (i - 1) + g + 1)
                    split_product(bank(H1_BANK, g), lambda p, k, b: (gw1_hi, gw1_lo)[p][:, k, half(b)],
                                  lambda p, k: (y_hi, y_lo)[p][:, g, k, :], S["h1_ps"])
                for g in range(2):
                    pe.wait_ge(S["h1_sb"], 2 * i + g + 1)
                    if is_first(i):
                        pe.wait_ge(S["b1_sb"], 1)
                    elif g == 0:
                        pe.wait_ge(S["prefix_read"], i)
                    product(bank(S2_BANK, g), lambda k, b: h1_t[:, g, k, half(b)],
                            lambda k: gw2_sb[:, k, :], S["s2_ps"])
                for g in range(2):
                    pe.wait_ge(S["adj_lo"], 2 * i + g + 1)
                    pe.wait_ge(S["s2_lo"], 2 * i + g + 1)
                    split_product(bank(H2_BANK, g), lambda p, k, b: (s2_hi, s2_lo)[p][:, g, k, half(b)],
                                  lambda p, k: (adj_hi, adj_lo)[p][:, g, k, :], S["h2_ps"])
                for g in range(2):
                    pe.wait_ge(S["h2_sb"], 2 * i + g + 1)
                    product(bank(S3_BANK, g), lambda k, b: h2_t[:, g, k, half(b)],
                            lambda k: gw3_sb[:, k, :], S["s3_ps"])
                if not is_last(i, PAIRS):
                    adjacencies_in(i + 1)
                if not is_first(i):
                    prefix(i - 1)
                for g in range(2):
                    pe.wait_ge(S["s3_lo"], 2 * i + g + 1)
                    split_product(bank(O3_BANK, g), lambda p, k, b: (adj_hi, adj_lo)[p][:, g, k, half(b)],
                                  lambda p, k: (s3_hi, s3_lo)[p][:, g, k, :], S["o3_ps"])
            pairs(pe, pair_of_graphs)
            prefix(PAIRS - 1)
            pe.wait_ge(S["run_made"], PAIRS)
            nc.tensor.matmul(COUNTS, ones_b[:, :], run_cnt[:, :], start=True, stop=True).then_inc(S["total_ps"], 1)
            pe.wait_ge(S["widths_made"], 1)
            passed(pe)

            def rows_in(j, u):
                pe.wait_ge(xr_loaded[u], 32 * (j + 1))
                if not (is_first(j) and u == 0):
                    pe.wait_ge(S["xt_sb"], U * j + u)
                for c, m in blocks(CAP):
                    for k in range(KD):
                        last = nc.tensor.transpose(XT_BANKS[:, k, c * P:c * P + m], xr[0:m, u, c, half(k)],
                                                   ident[0:m, 0:m])
                last.then_inc(S["xt_ps"], 1)

            def up(j, u, w):
                i = U * j + u
                pe.wait_ge(w1_loaded[u], 16 * (j + 1))
                pe.wait_ge(S["xt_sb"], i + 1)
                for f in range(JF):
                    if w > PLAIN:
                        pe.wait_ge(S["w1_lo"], 4 * i + f // 2 + 1)
                    if not (is_first(j) and u == 0 and f < H_BANKS):
                        pe.wait_ge(S["gelu_done"], JF * i + f + 1 - H_BANKS)
                    to = ps[:, H_BANK + f % H_BANKS, 0:w]
                    if w > PLAIN:
                        parts = [(wp[:, u % 2, k, half(f)], xp[:, u % 2, k, 0:w]) for k in range(KD)
                                 for wp, xp in ((w1_hi, xt_hi), (w1_hi, xt_lo), (w1_lo, xt_hi))]
                    else:
                        parts = [(w1_sb[:, u, k, half(f)], xt[:, u % 2, k, 0:w]) for k in range(KD)]
                    for at, (lhs, rhs) in enumerate(parts):
                        last = nc.tensor.matmul(to, lhs, rhs, start=(at == 0), stop=(at == len(parts) - 1))
                    last.then_inc(S["hid_ps"], 1)

            def down(j, u, w):
                i = U * j + u
                if not (is_first(j) and u == 0):
                    pe.wait_ge(S["y_made"], i)
                for c, m in blocks(w):
                    for f in range(JF):
                        if c == 0 and f % (JF // 2) == 0:
                            pe.wait_ge(w2_lo[f // (JF // 2)], i + 1)
                        if c == 0 and f % 2 == 0:
                            pe.wait_ge(S["hid_lo"], JF // 2 * i + f // 2 + 1)
                        for at, (hp, wp) in enumerate(((h_hi, w2_hi), (h_hi, w2_low), (h_lo, w2_hi))):
                            last = nc.tensor.matmul(y_bank(c, m), hp[:, f, c * P:c * P + m],
                                                    wp[:, u % 2, f, :], start=(f == 0 and at == 0),
                                                    stop=(f == JF - 1 and at == 2))
                last.then_inc(S["down_done"], 1)

            rows_in(0, 0)
            rows_in(0, 1)

            def round_of_products(j):
                four = nc.values_load_multi_w_load_instructions(
                    round_widths[0:1, bass.ds(j, 1)], engines=(mybir.EngineType.PE,), min_val=0, max_val=4**U - 1)[1][0]
                for u in range(U):
                    width = (four >> (2 * u)) & 3
                    def body(w):
                        up(j, u, w)
                        if not (is_last(j, E // U) and u >= 2):
                            rows_in(*later(j, u, 2))
                        down(j, u, w)
                    with pe.If(width < 1):
                        body(WIDTHS[0])
                    with pe.Else():
                        with pe.If(width < 3):
                            with pe.If(width < 2):
                                body(WIDTHS[1])
                            with pe.Else():
                                body(WIDTHS[2])
                        with pe.Else():
                            body(WIDTHS[3])
            rounds(pe, round_of_products)


_INS = ['x', 'adj', 'L0_gnn_W1', 'L0_gnn_b1', 'L0_gnn_W2', 'L0_gnn_b2', 'L0_gnn_W3', 'L0_gnn_b3',
        'L0_ffn_W_hash', 'L0_ffn_W1', 'L0_ffn_b1', 'L0_ffn_W2', 'L0_ffn_b2']
_OUTS = [((32 * 256 + 384, 256), 'float32')]


def kernel(**inputs):
    import numpy as _np
    import concourse.bacc as _bacc
    from concourse import mybir as _mybir
    from concourse.bass_utils import run_bass_kernel_spmd as _run

    nc = _bacc.Bacc("TRN2", target_bir_lowering=False, num_devices=1)
    arrays, args = {}, []
    for name in _INS:
        a = _np.ascontiguousarray(inputs[name])
        arrays[f"in_{name}_dram"] = a
        args.append(nc.dram_tensor(f"in_{name}_dram", a.shape, _mybir.dt.from_np(a.dtype), kind="ExternalInput").ap())
    for i, (shape, dtype) in enumerate(_OUTS):
        dt = _mybir.dt.from_np(_np.dtype(dtype))
        args.append(nc.dram_tensor(f"out_{i}_dram", shape, dt, kind="ExternalOutput").ap())
    gnn_then_hash_routed_experts(nc, *args)
    r = _run(nc, [arrays], core_ids=[0])
    got = tuple(r.results[0][f"out_{i}_dram"] for i in range(len(_OUTS)))
    return got[0][:32 * 256].reshape(32, 256, 256)
```
